# Optimizing a Trainium2 kernel written in Bass

```python
import numpy as np
import jax
import jax.numpy as jnp

def _softmax(x, axis=-1):
    return jax.nn.softmax(x, axis=axis)

def _gelu(x):
    return jax.nn.gelu(x, approximate=True)

def _silu(x):
    return jax.nn.silu(x)

def _sigmoid(x):
    return jax.nn.sigmoid(x)

def _layernorm(x, axis=-1, eps=1e-05):
    m = jnp.mean(x, axis=axis, keepdims=True)
    v = jnp.var(x, axis=axis, keepdims=True)
    return (x - m) / jnp.sqrt(v + eps)

def _scatter_add(tgt, idx, src, axis=0):
    return tgt.at[idx].add(src)

def _segment_sum(src, seg, n):
    return jax.ops.segment_sum(src, seg, n)
kernel_name = 'mk_lm_tower_d1_tok_ids512_r4_2b10d1'

def setup_inputs(seed: int=0):
    np.random.seed(seed)
    _w = jnp.asarray

    def _rec_inputs():
        import jax
        import jax.numpy as jnp
        _rk = jax.random.key(seed)
        x = jax.random.randint(jax.random.fold_in(_rk, 1), (32, 512), 0, 12564, jnp.int32)
        return x
    x = _rec_inputs()

    def _L0_tok_setup():
        import jax, jax.numpy as jnp
        import numpy as np
        VOCAB, D, B, S, E = (50257, 128, 8, 512, 5)
        L_CONST = 1000000000.0
        key = jax.random.key(seed)
        k = jax.random.split(key, 5)
        return {'input_ids': jax.random.randint(k[0], (B, S), 0, VOCAB, dtype=jnp.int64), 'emb_table': jax.random.normal(k[1], (VOCAB, D), dtype=jnp.float32), 'gate_table': jax.random.uniform(k[2], (VOCAB, 1), dtype=jnp.float32, minval=0.001, maxval=1.0), 'expert_w': jax.random.normal(k[3], (E, D, D), dtype=jnp.float32) * 0.02, 'expert_b': jax.random.normal(k[4], (E, D), dtype=jnp.float32) * 0.02}
    _L0_tok_all = _L0_tok_setup()
    _L0_tok_in = {k: v for k, v in _L0_tok_all.items() if k in ('emb_table', 'gate_table', 'expert_w', 'expert_b')}
    del _L0_tok_all

    def _L0_attn_setup():
        import jax, jax.numpy as jnp
        import numpy as np
        B, S, D = (8, 512, 128)
        key = jax.random.key(seed)
        k1, k2 = jax.random.split(key)
        lstm_out = jax.random.normal(k1, (B, S, D), dtype=jnp.float32)
        limit = float(np.sqrt(6.0 / (D + D)))
        attention_weights = jax.random.uniform(k2, (D, D), dtype=jnp.float32, minval=-limit, maxval=limit)
        return {'lstm_out': lstm_out, 'attention_weights': attention_weights}
    _L0_attn_all = _L0_attn_setup()
    _L0_attn_in = {k: v for k, v in _L0_attn_all.items() if k in ('attention_weights',)}
    del _L0_attn_all

    def _L0_ffn_setup():
        import jax, jax.numpy as jnp
        import numpy as np
        B, T, D, H = (64, 128, 128, 256)

        def _linear_params(key, out_dim, in_dim):
            kw, kb = jax.random.split(key)
            bound = 1.0 / np.sqrt(in_dim)
            W = jax.random.uniform(kw, (out_dim, in_dim), jnp.float32, -bound, bound)
            b = jax.random.uniform(kb, (out_dim,), jnp.float32, -bound, bound)
            return (W, b)
        key = jax.random.key(seed)
        ks = jax.random.split(key, 8)
        x = jax.random.normal(ks[0], (B, T, D), jnp.float32)
        Wuz, buz = _linear_params(ks[1], H, D)
        Wwz, bwz = _linear_params(ks[2], H, H)
        Wur, bur = _linear_params(ks[3], H, D)
        Wwr, bwr = _linear_params(ks[4], H, H)
        Wu, bu = _linear_params(ks[5], H, D)
        Ww, bw = _linear_params(ks[6], H, H)
        Wo, bo = _linear_params(ks[7], D, H)
        return dict(x=x, Wuz=Wuz, buz=buz, Wwz=Wwz, bwz=bwz, Wur=Wur, bur=bur, Wwr=Wwr, bwr=bwr, Wu=Wu, bu=bu, Ww=Ww, bw=bw, Wo=Wo, bo=bo)
    _L0_ffn_all = _L0_ffn_setup()
    _L0_ffn_in = {k: v for k, v in _L0_ffn_all.items() if k in ('Wuz', 'buz', 'Wwz', 'bwz', 'Wur', 'bur', 'Wwr', 'bwr', 'Wu', 'bu', 'Ww', 'bw', 'Wo', 'bo')}
    del _L0_ffn_all
    return {'x': x, 'L0_tok_emb_table': _L0_tok_in['emb_table'], 'L0_tok_gate_table': _L0_tok_in['gate_table'], 'L0_tok_expert_w': _L0_tok_in['expert_w'], 'L0_tok_expert_b': _L0_tok_in['expert_b'], 'L0_attn_attention_weights': _L0_attn_in['attention_weights'], 'L0_ffn_Wuz': _L0_ffn_in['Wuz'], 'L0_ffn_buz': _L0_ffn_in['buz'], 'L0_ffn_Wwz': _L0_ffn_in['Wwz'], 'L0_ffn_bwz': _L0_ffn_in['bwz'], 'L0_ffn_Wur': _L0_ffn_in['Wur'], 'L0_ffn_bur': _L0_ffn_in['bur'], 'L0_ffn_Wwr': _L0_ffn_in['Wwr'], 'L0_ffn_bwr': _L0_ffn_in['bwr'], 'L0_ffn_Wu': _L0_ffn_in['Wu'], 'L0_ffn_bu': _L0_ffn_in['bu'], 'L0_ffn_Ww': _L0_ffn_in['Ww'], 'L0_ffn_bw': _L0_ffn_in['bw'], 'L0_ffn_Wo': _L0_ffn_in['Wo'], 'L0_ffn_bo': _L0_ffn_in['bo']}

def reference(x, L0_tok_emb_table, L0_tok_gate_table, L0_tok_expert_w, L0_tok_expert_b, L0_attn_attention_weights, L0_ffn_Wuz, L0_ffn_buz, L0_ffn_Wwz, L0_ffn_bwz, L0_ffn_Wur, L0_ffn_bur, L0_ffn_Wwr, L0_ffn_bwr, L0_ffn_Wu, L0_ffn_bu, L0_ffn_Ww, L0_ffn_bw, L0_ffn_Wo, L0_ffn_bo):
    import jax
    import jax.numpy as jnp

    def _L0_tok_ref(input_ids, emb_table, gate_table, expert_w, expert_b):
        import jax, jax.numpy as jnp
        import numpy as np
        VOCAB, D, B, S, E = (50257, 128, 8, 512, 5)
        L_CONST = 1000000000.0
        d = emb_table.shape[1]
        n_exp = expert_w.shape[0]
        data = emb_table[input_ids]
        gate = gate_table[input_ids] * d
        idx_arr = jnp.arange(d, dtype=gate.dtype)
        frac = (L_CONST * gate - jnp.floor(L_CONST * gate)) / L_CONST
        mask = (idx_arr[None, None, :] < gate).astype(gate.dtype) + frac
        divisor = float(d // n_exp)
        eidx = jnp.clip(jnp.floor_divide(mask.sum(-1), divisor).astype(jnp.int32), 0, n_exp - 1)
        xm = data * mask
        y_all = jnp.einsum('bsd,eod->bseo', xm, expert_w) + expert_b[None, None]
        onehot = jax.nn.one_hot(eidx, n_exp, dtype=xm.dtype)
        return jnp.einsum('bseo,bse->bso', y_all, onehot)

    def _L0_attn_ref(lstm_out, attention_weights):
        import jax, jax.numpy as jnp
        import numpy as np
        B, S, D = (8, 512, 128)
        proj = jnp.einsum('bsd,de->bse', lstm_out, attention_weights)
        scores = jnp.tanh(jnp.einsum('bsd,btd->bst', proj, lstm_out))
        attn = jax.nn.softmax(scores, axis=-1)
        return jnp.einsum('bst,btd->bsd', attn, lstm_out)

    def _L0_ffn_ref(x, Wuz, buz, Wwz, bwz, Wur, bur, Wwr, bwr, Wu, bu, Ww, bw, Wo, bo):
        import jax, jax.numpy as jnp
        import numpy as np
        B, T, D, H = (64, 128, 128, 256)

        def _linear_params(key, out_dim, in_dim):
            kw, kb = jax.random.split(key)
            bound = 1.0 / np.sqrt(in_dim)
            W = jax.random.uniform(kw, (out_dim, in_dim), jnp.float32, -bound, bound)
            b = jax.random.uniform(kb, (out_dim,), jnp.float32, -bound, bound)
            return (W, b)
        b_, t_, _ = x.shape
        h_dim = Wwz.shape[0]
        xz = (jnp.einsum('btd,hd->bth', x, Wuz) + buz).transpose(1, 0, 2)
        xr = (jnp.einsum('btd,hd->bth', x, Wur) + bur).transpose(1, 0, 2)
        xc = (jnp.einsum('btd,hd->bth', x, Wu) + bu).transpose(1, 0, 2)

        def step(h, inp):
            xz_t, xr_t, xc_t = inp
            z = jax.nn.sigmoid(xz_t + h @ Wwz.T + bwz)
            r = jax.nn.sigmoid(xr_t + h @ Wwr.T + bwr)
            c = jnp.tanh(xc_t + h * r @ Ww.T + bw)
            h_new = z * h + (1.0 - z) * c
            return (h_new, h_new)
        h0 = jnp.zeros((b_, h_dim), x.dtype)
        _, hs = jax.lax.scan(step, h0, (xz, xr, xc))
        out = jax.nn.sigmoid(jnp.einsum('tbh,dh->btd', hs, Wo) + bo)
        return out
    h = _L0_tok_ref(x, L0_tok_emb_table, L0_tok_gate_table, L0_tok_expert_w, L0_tok_expert_b)
    h = h + _L0_attn_ref(_layernorm(h, axis=-1), L0_attn_attention_weights)
    h = h + _L0_ffn_ref(_layernorm(h, axis=-1), L0_ffn_Wuz, L0_ffn_buz, L0_ffn_Wwz, L0_ffn_bwz, L0_ffn_Wur, L0_ffn_bur, L0_ffn_Wwr, L0_ffn_bwr, L0_ffn_Wu, L0_ffn_bu, L0_ffn_Ww, L0_ffn_bw, L0_ffn_Wo, L0_ffn_bo)
    return h

_drawn_inputs = setup_inputs


def setup_inputs(seed=0):
    import zlib

    import numpy as np

    out = dict(_drawn_inputs(seed))
    spreads = {}
    factors = {'L0_ffn_Wuz': 3.051,
     'L0_ffn_buz': 27.833,
     'L0_ffn_Wwz': 8.0,
     'L0_ffn_bwz': 36.981,
     'L0_ffn_Wur': 8.0,
     'L0_ffn_bur': 43.791,
     'L0_ffn_Wwr': 8.0,
     'L0_ffn_bwr': 62.123,
     'L0_ffn_bu': 5.876,
     'L0_ffn_Ww': 2.924,
     'L0_ffn_bw': 7.62,
     'L0_ffn_bo': 3.236}
    for name, (base, spread) in spreads.items():
        noise = np.random.default_rng([zlib.crc32(name.encode()), seed]).standard_normal(out[name].shape)
        drawn = base * np.exp(spread * noise) if base else spread * noise
        out[name] = jnp.asarray(drawn.astype(out[name].dtype))
    for name, factor in factors.items():
        out[name] = (out[name] * factor).astype(out[name].dtype)
    return out
```

```python
from contextlib import ExitStack

import concourse.bass as bass
from concourse import mybir

F32 = mybir.dt.float32
F16 = mybir.dt.float16
BF16 = mybir.dt.bfloat16
I32 = mybir.dt.int32
U32 = mybir.dt.uint32
ALU = mybir.AluOpType
ACT = mybir.ActivationFunctionType
AX_X = mybir.AxisListType.X
RMAX = bass.bass_isa.ReduceOp.max

P = 128
B, S, D, H, E = 32, 512, 128, 256, 5
T = S // P
ROW = D + 1
KC = H // P
GS = 4
GC = GS * B
BODY = 2 * GS
BIG = float(2 ** 23)
L_CONST = 1e9
EXPERT_SPAN = D // E
EXPERT_FROM = [float(EXPERT_SPAN * e - 1) for e in range(E)]
EPS = 1e-5
SMALLEST_SCALE = 2.0 ** -12
EXPONENT_BITS = 0x7F800000


def tower_kernel(nc, x_cols, table, expert_wT, expert_b, attn_w, wxT, bx, bh, whT, woT, bo, consts, out):
    h2_dram = nc.dram_tensor("residual_scratch", (B, S, D), F32, kind="Internal").ap()

    with ExitStack() as ctx:
        def sb(name, shape, dt=F32):
            return ctx.enter_context(nc.sbuf_tensor(name, shape, dt))

        def sem(name):
            return ctx.enter_context(nc.semaphore(name))

        bank = [ctx.enter_context(nc.psum_tensor(f"bank{i}", [P, 512], F32)) for i in range(8)]

        const = sb("const", [P, 2 * P + 7])
        ident, unit = const[:, 0:P], const[:, P:2 * P]
        row_from = const[:, 2 * P:2 * P + 1]
        exp_part = [const[:, 2 * P + 1 + i:2 * P + 2 + i] for i in range(3)]
        one_part = [const[:, 2 * P + 4 + i:2 * P + 5 + i] for i in range(3)]
        ones16 = sb("ones16", [P, P], BF16)
        token_id = sb("token_id", [P, B * T], I32)
        w_expert = sb("w_expert", [P, E, D])
        w_expert_in = sb("w_expert_in", [P, E, D])
        w_attn = sb("w_attn", [P, D])
        w_x = sb("w_x", [P, 3, H])
        w_h_in = sb("w_h_in", [P, 3, KC, H])
        w_h = sb("w_h", [P, 2, 3, KC, H], F16)
        w_o_in = sb("w_o_in", [P, KC, D])
        w_o = sb("w_o", [P, KC, D])
        NBIAS = 3 * H + 2 * D
        bias_in = sb("bias_in", [P, NBIAS])
        bias_less = sb("bias_less", [P, NBIAS])
        bias_rest = sb("bias_rest", [P, 3, NBIAS])
        bias_part = sb("bias_part", [P, 3, NBIAS], BF16)
        bias_sum = sb("bias_sum", [P, 3, NBIAS], BF16)
        bias_x, bias_o = bias_sum[:, 2, 0:3 * H], bias_sum[:, 2, 3 * H:3 * H + D]
        bias_e = bias_sum[:, 2, 3 * H + D:NBIAS]
        scales = sb("scales", [P, 8])
        w_max, w_min, w_abs, w_all, w_clamp, h_scale, h_scale2, w_scale = (scales[:, i:i + 1] for i in range(8))
        neg_h_scale = sb("neg_h_scale", [P, 1])

        ids_now = sb("ids_now", [P, 2, T], I32)
        emb = sb("emb", [P, 2, T, ROW])
        gate = sb("gate", [P, 2, T])
        frac = sb("frac", [P, 2, T])
        gwork = sb("gwork", [P, 8, T])
        mask = sb("mask", [P, T, P])
        xm = sb("xm", [P, T, P])
        xmT = sb("xmT", [P, T * P])
        kept = sb("kept", [P, E - 1, T * P])
        bias_row = sb("bias_row", [P, T * P], BF16)
        h1 = sb("h1", [P, 2, T, P])
        stat1, stat2 = sb("stat1", [P, T, 6]), sb("stat2", [P, T, 6])
        mv1, mv2 = sb("mv1", [P, T, 2]), sb("mv2", [P, T, 2])
        var1, var2 = sb("var1", [P, T]), sb("var2", [P, T])
        rstd1, rstd2 = sb("rstd1", [P, T]), sb("rstd2", [P, T])
        minus_half = sb("minus_half", [P, T])
        xn = sb("xn", [P, 2, T, ROW])
        xnT = sb("xnT", [P, T * P])
        projT = sb("projT", [P, T * P])
        th = sb("th", [P, 2, T * P])
        ex = sb("ex", [P, T, T * P])
        rsum = sb("rsum", [P, T])
        h2 = sb("h2", [P, 2, T, P])
        xf = sb("xf", [P, T, P])
        scan_x = sb("scan_x", [P, (S + GS) * B])

        h32 = sb("h32", [P, KC, BODY * B])
        h_a, h_b = sb("h_a", [P, KC, B], F16), sb("h_b", [P, KC, B], F16)
        r, z, c = sb("r", [P, KC, B]), sb("z", [P, KC, B]), sb("c", [P, KC, B])
        rh, rh_a, rh_b = sb("rh", [P, KC, B]), sb("rh_a", [P, KC, B], F16), sb("rh_b", [P, KC, B], F16)
        zh, zh_a, zh_b = sb("zh", [P, KC, B]), sb("zh_a", [P, KC, B], F16), sb("zh_b", [P, KC, B], F16)
        omz = sb("omz", [P, KC, B])
        u, u_a, u_b = sb("u", [P, KC, B]), sb("u_a", [P, KC, B], F16), sb("u_b", [P, KC, B], F16)
        res = sb("res", [P, 2, D])
        sig = sb("sig", [P, 2, D])
        fin = sb("fin", [P, 2, D])

        s_in, s_small, s_wh, s_bias = sem("s_in"), sem("s_small"), sem("s_wh"), sem("s_bias")
        s_zero, s_dve, s_pool0, s_ready = sem("s_zero"), sem("s_dve"), sem("s_pool0"), sem("s_ready")
        front = {n: sem("f_" + n) for n in (
            "ids", "gate0", "gate", "mask", "xm", "xm_t", "gate_t", "xmT", "kept", "bias_row", "y", "h1", "bn1",
            "mv1", "var1", "rstd1", "xn", "xn_t", "xnT", "proj", "projT", "att", "rsum", "h2", "bn2", "mv2", "var2",
            "rstd2", "xf", "xf_t", "scan_x")}
        f_emb = [sem(f"f_emb{i}") for i in range(2)]
        f_store = [sem(f"f_store{i}") for i in range(2)]
        f_score = [sem(f"f_score{t}") for t in range(T)]
        f_tanh = [sem(f"f_tanh{t}") for t in range(T)]
        f_exp = [sem(f"f_exp{t}") for t in range(T)]
        g = {n: sem("g_" + n) for n in (
            "r_pre", "z_pre", "c_pre", "r", "z", "c", "rh", "rh_a", "rh_b", "zh", "zh_a", "zh_b", "omz",
            "u", "u_a", "u_b", "h", "h_a", "h_b", "o_pre", "o_sig", "o_fin")}
        o_res = [sem(f"o_res{i}") for i in range(2)]
        o_store = [sem(f"o_store{i}") for i in range(2)]

        tT, gT, sc, y_bank, o_bank, misc = bank[0], bank[1], bank[2:4], bank[4], bank[5:7], bank[7]
        pre_r = [bank[i][:, 0:KC * GC].rearrange("p (m n) -> p m n", m=KC) for i in (0, 1)]
        pre_z = [bank[i][:, 0:KC * GC].rearrange("p (m n) -> p m n", m=KC) for i in (2, 3)]
        pre_c = [bank[i][:, 0:KC * GC].rearrange("p (m n) -> p m n", m=KC) for i in (4, 5)]
        pre_o = [bank[i][:, 0:D] for i in (6, 7)]

        def rows(eng, base):
            if isinstance(base, int):
                return lambda k: base + k
            cache = {}

            def at(k):
                if k not in cache:
                    cache[k] = eng.snap(base + k)
                return cache[k]
            return at

        def wait(eng, s, value):
            if not (isinstance(value, int) and value <= 0):
                eng.wait_ge(s, value)

        def wait_apart(eng, s, value, constants, count):
            if not isinstance(value, int):
                value = eng.to_reg(value)
            eng.wait_ge(constants, count)
            wait(eng, s, value)

        def landed(eng, i, at):
            base = at(0)
            if isinstance(base, int):
                return 16 * T * (base // 2 + 1)
            return eng.snap((base - i % 2) * (8 * T) + 16 * T)

        def gate_steps(eng, at, per_row, k):
            base = at(0)
            return base * per_row + k if isinstance(base, int) else eng.snap(base * per_row + k)

        def stored(eng, i, at):
            base = at(0)
            if isinstance(base, int):
                return 16 * (base // 2)
            return eng.snap((base - i % 2) * 8)

        def front_schedule(eng, stages):
            for i in range(-1, 4):
                stages(i, rows(eng, i))
            with eng.Fori(2, B // 2 - 1) as n:
                for p in range(2):
                    at = rows(eng, eng.snap(n * 2 + p))
                    stages(2 + p, at)
            for i in (B - 2, B - 1):
                stages(i, rows(eng, i))
            stages(B, rows(eng, B))

        def scan_schedule(eng, body):
            for n in range(2):
                body(rows(eng, n * BODY), rows(eng, n * 2), rows(eng, n * 16), n == 0)
            with eng.Fori(2, S // BODY) as n:
                body(rows(eng, eng.snap(n * BODY)), rows(eng, eng.snap(n * 2)), rows(eng, eng.snap(n * 16)), False)

        block = ctx.enter_context(nc.Block())

        @block.sync
        def _(sp):
            sp.dma_start(token_id[:], x_cols).then_inc(s_in, 16)
            sp.dma_start(const[:], consts).then_inc(s_in, 16)
            sp.dma_start(w_expert_in[:], expert_wT).then_inc(s_in, 16)
            sp.dma_start(w_attn[:], attn_w).then_inc(s_in, 16)
            sp.dma_start(w_x[:], wxT).then_inc(s_small, 16)
            sp.dma_start(w_h_in[:], whT).then_inc(s_wh, 16)
            sp.dma_start(w_o_in[:], woT).then_inc(s_wh, 16)
            sp.wait_ge(s_zero, 2)
            xo = slice(3 * H, 3 * H + D)
            xe = slice(3 * H + D, NBIAS)
            for i in range(3):
                sp.dma_start(bias_in[i:i + 1, 0:3 * H], bx).then_inc(s_bias, 16)
                sp.dma_start(bias_less[i:i + 1, 0:3 * H], bh).then_inc(s_bias, 16)
                sp.dma_start(bias_in[i:i + 1, xo], bo).then_inc(s_bias, 16)
                sp.dma_start(bias_in[E * i:E * i + E, xe], expert_b).then_inc(s_bias, 16)
                sp.dma_start(bias_less[E * i + 1:E * i + E, xe], expert_b[0:E - 1, :]).then_inc(s_bias, 16)

            def store_residual(i, at):
                if 0 <= i < B:
                    sp.wait_ge(front["h2"], at(1))
                    dst = h2_dram[bass.ds(at(0), 1), :, :].rearrange("b (j p) d -> p (b j) d", p=P)
                    sp.dma_start(dst, h2[:, i % 2]).then_inc(f_store[i % 2], 16)

            front_schedule(sp, store_residual)
            for i in range(2):
                sp.wait_ge(f_store[i], 16 * (B // 2))

            def rows_of(dram, at, q):
                return dram.rearrange("b s d -> s b d")[bass.ds(at(GS * q), GS), :, :]

            def results(at, group, load, first):
                for q in range(2):
                    if not first:
                        sp.wait_ge(g["o_fin"], group(q - 1))
                        sp.dma_start(rows_before(out, at, q), fin[:, q]).then_inc(o_store[q], 16)
                    sp.dma_start(res[:, q], rows_of(h2_dram, at, q)).then_inc(o_res[q], 16)

            def rows_before(dram, at, q):
                return dram.rearrange("b s d -> s b d")[bass.ds(at(GS * q - BODY), GS), :, :]

            scan_schedule(sp, results)
            for q in range(2):
                sp.wait_ge(g["o_fin"], S // GS - 1 + q)
                sp.dma_start(rows_of(out, lambda k: S - BODY + k, q), fin[:, q]).then_inc(o_store[q], 16)
            for q in range(2):
                sp.wait_ge(o_store[q], 16 * (S // BODY))

        @block.gpsimd
        def _(pool):
            nc.gpsimd.memset(minus_half[:], -0.5).then_inc(s_pool0, 1)
            pool.wait_ge(s_in, 64)

            def gather(i, at):
                q = i % 2
                nc.gpsimd.tensor_copy(ids_now[:, q], token_id[:, bass.ds(at(0) * T, T)]).then_inc(front["ids"], 1)
                wait_apart(pool, front["ids"], at(1), s_pool0, 1)
                wait(pool, front["xm"], at(-1))
                for j in range(T):
                    sent = nc.gpsimd.indirect_dma_start(
                        out=emb[:, q, j, :], out_offset=None, in_=table,
                        in_offset=bass.IndirectOffsetOnAxis(ap=ids_now[:, q, j:j + 1].bitcast(U32), axis=0))
                    sent.then_inc(f_emb[q], 16)

            chain = [0]

            def gates(i, at):
                q = i % 2
                lands = landed(pool, i, at)
                wait_apart(pool, f_emb[q], lands, s_pool0, 1)
                wait(pool, front["kept"], at(-1))
                ts, tt, w = nc.gpsimd.tensor_scalar, nc.gpsimd.tensor_tensor, gwork
                steps = [
                    lambda: ts(gate[:, q], emb[:, q, :, D], float(D), None, ALU.mult),
                    lambda: ts(w[:, 0], gate[:, q], L_CONST, BIG, ALU.mult, ALU.min),
                    lambda: ts(w[:, 1], w[:, 0], -BIG, None, ALU.max),
                    lambda: ts(w[:, 2], w[:, 1], 0.0, BIG, ALU.max, ALU.add),
                    lambda: ts(w[:, 3], w[:, 1], 0.0, -BIG, ALU.min, ALU.add),
                    lambda: ts(w[:, 3], w[:, 3], BIG, None, ALU.add),
                    lambda: ts(w[:, 2], w[:, 2], -BIG, None, ALU.add),
                    lambda: tt(w[:, 4], w[:, 2], w[:, 3], ALU.add),
                    lambda: tt(w[:, 5], w[:, 4], w[:, 1], ALU.subtract),
                    lambda: ts(w[:, 6], w[:, 5], 0.0, None, ALU.is_gt),
                    lambda: tt(w[:, 7], w[:, 6], w[:, 5], ALU.subtract),
                    lambda: ts(frac[:, q], w[:, 7], 1.0 / L_CONST, None, ALU.mult),
                ]
                for k, step in enumerate(steps):
                    step().then_inc(front["gate0"] if k < len(steps) - 1 else front["gate"], 1)
                    if k < len(steps) - 1:
                        wait_apart(pool, front["gate0"], gate_steps(pool, at, len(steps) - 1, k + 1), s_pool0, 1)

            def power(i, at, var, rstd, which, reader):
                pool.wait_ge(front["var" + which], at(1))
                wait(pool, front[reader], at(0))
                nc.gpsimd.tensor_tensor(rstd[:], var[:], minus_half[:], ALU.pow).then_inc(front["rstd" + which], 1)

            def stages(i, at):
                nxt = lambda k: at(k + 1)
                if i + 1 < B:
                    if i == -1:
                        gather(0, nxt)
                    gates(i + 1, nxt)
                    if i + 2 < B:
                        gather(i + 2, lambda k: at(k + 2))
                if 1 <= i:
                    power(i - 1, lambda k: at(k - 1), var2, rstd2, "2", "xf")
                if i + 1 < B:
                    power(i + 1, nxt, var1, rstd1, "1", "xn")

            pool.wait_ge(s_pool0, 1)
            pool.wait_ge(s_dve, 2)
            nc.gpsimd.partition_all_reduce(w_all, w_abs, P, RMAX).then_inc(s_pool0, 1)
            front_schedule(pool, stages)

            def results(at, group, load, first):
                for q in range(2):
                    if not (first and q == 0):
                        output(group(q), load, q)

            def output(count, load, q):
                o = 1 - q
                pool.wait_ge(g["o_sig"], count)
                pool.wait_ge(o_res[o], load(16 if o == 0 else 0))
                wait(pool, o_store[o], load(0 if o == 0 else -16))
                nc.gpsimd.tensor_tensor(fin[:, o], sig[:, o], res[:, o], ALU.add).then_inc(g["o_fin"], 1)

            scan_schedule(pool, results)
            output(S // GS, lambda k: 16 * (S // BODY) + k, 0)

        @block.scalar
        def _(act):
            def copy(dst, src, s):
                nc.scalar.copy(dst, src).then_inc(s, 1)

            def stages(i, at):
                if 0 <= i < B:
                    act.wait_ge(front["xn_t"], at(1))
                    wait(act, front["att"], at(0))
                    copy(xnT[:], misc[:], front["xnT"])
                if i + 1 < B:
                    act.wait_ge(front["xm_t"], at(2))
                    wait(act, front["y"], at(1))
                    copy(xmT[:], tT[:], front["xmT"])
                if 0 <= i < B:
                    act.wait_ge(front["proj"], at(1))
                    copy(projT[:], sc[1][:], front["projT"])
                    for t in range(T + 1):
                        if t < T:
                            act.wait_ge(f_score[t], at(1))
                            if t >= 2:
                                act.wait_ge(f_exp[t - 2], at(1))
                            else:
                                wait(act, f_exp[t + 2], at(0))
                            nc.scalar.activation(th[:, t % 2], sc[t % 2][:], ACT.Tanh).then_inc(f_tanh[t], 1)
                        if t >= 1:
                            act.wait_ge(f_tanh[t - 1], at(1))
                            wait(act, front["att"], at(0))
                            nc.scalar.activation(ex[:, t - 1], th[:, (t - 1) % 2], ACT.Exp).then_inc(f_exp[t - 1], 1)
                if 1 <= i:
                    act.wait_ge(front["xf_t"], at(0))
                    dst = scan_x[:, 0:S * B].rearrange("p (s b) -> p s b", b=B)[:, :, bass.ds(at(-1), 1)]
                    copy(dst.rearrange("p s b -> p (s b)"), misc[:], front["scan_x"])
                if i + 1 < B:
                    act.wait_ge(front["y"], at(2))
                    if i >= 1:
                        act.wait_ge(front["h2"], at(0))
                    copy(h1[:, (i + 1) % 2].rearrange("p t d -> p (t d)"), y_bank[:], front["h1"])

            front_schedule(act, stages)

            def scan(at, group, load, first):
                for s in range(BODY):
                    q, k = s // GS, s % GS * B
                    now = at(s + 1)
                    act.wait_ge(g["r_pre"], now)
                    nc.scalar.activation(r[:], pre_r[q][:, :, k:k + B], ACT.Sigmoid).then_inc(g["r"], 1)
                    act.wait_ge(g["z_pre"], now)
                    nc.scalar.activation(z[:], pre_z[q][:, :, k:k + B], ACT.Sigmoid).then_inc(g["z"], 1)
                    act.wait_ge(g["z"], now)
                    nc.scalar.activation(omz[:], z[:], ACT.Identity, scale=neg_h_scale[:], bias=h_scale2).then_inc(g["omz"], 1)
                    act.wait_ge(g["c_pre"], now)
                    nc.scalar.activation(c[:], pre_c[q][:, :, k:k + B], ACT.Tanh).then_inc(g["c"], 1)
                    if s % GS == 1 and not (first and q == 0):
                        output(group(q), group(q - 2), q)

            def output(count, used, q):
                o = 1 - q
                act.wait_ge(g["o_pre"], count)
                wait(act, g["o_fin"], used)
                nc.scalar.activation(sig[:, o], pre_o[o], ACT.Sigmoid).then_inc(g["o_sig"], 1)

            scan_schedule(act, scan)
            output(S // GS, S // GS - 2, 0)

        @block.vector
        def _(dve):
            v = nc.vector
            done = [0]

            def then_wait(ins):
                done[0] += 1
                ins.then_inc(s_dve, 1)
                dve.wait_ge(s_dve, done[0])

            v.memset(bias_in[:], 0.0).then_inc(s_zero, 1)
            v.memset(bias_less[:], 0.0).then_inc(s_zero, 1)
            v.memset(scan_x[:, S * B:], 0.0).then_inc(s_ready, 1)
            v.memset(xn[:, :, :, D:ROW], 1.0).then_inc(s_ready, 1)
            dve.wait_ge(s_wh, 32)
            flat = w_h_in[:].rearrange("p a b c -> p (a b c)")
            v.tensor_reduce(w_max, flat, AX_X, ALU.max).then_inc(s_ready, 1)
            then_wait(v.tensor_reduce(w_min, flat, AX_X, ALU.min))
            dve.wait_ge(s_ready, 3)
            then_wait(v.scalar_tensor_tensor(out=w_abs, in0=w_min, scalar=-1.0, in1=w_max, op0=ALU.mult, op1=ALU.max))
            dve.wait_ge(s_in, 64)
            v.tensor_copy(w_expert[:, 0], w_expert_in[:, 0]).then_inc(s_ready, 1)
            v.tensor_tensor(w_expert[:, 1:E], w_expert_in[:, 1:E], w_expert_in[:, 0:E - 1], ALU.subtract).then_inc(s_ready, 1)
            xb = slice(0, 3 * H + D)
            xe = slice(3 * H + D, NBIAS)
            dve.wait_ge(s_bias, 16 * 15)
            v.tensor_tensor(bias_rest[:, 0, xb], bias_in[:, xb], bias_less[:, xb], ALU.add).then_inc(s_ready, 1)
            then_wait(v.tensor_tensor(bias_rest[:, 0, xe], bias_in[:, xe], bias_less[:, xe], ALU.subtract))
            dve.wait_ge(s_ready, 6)
            for k in range(3):
                then_wait(v.tensor_copy(bias_part[:, k], bias_rest[:, k]))
                if k < 2:
                    then_wait(v.tensor_tensor(bias_rest[:, k + 1], bias_rest[:, k], bias_part[:, k], ALU.subtract))
            for cols, pick in ((xb, one_part), (xe, exp_part)):
                then_wait(v.tensor_scalar(bias_sum[:, 0, cols], bias_part[:, 0, cols], pick[0], None, ALU.mult))
                for k in (1, 2):
                    then_wait(v.scalar_tensor_tensor(out=bias_sum[:, k, cols], in0=bias_part[:, k, cols], scalar=pick[k],
                                                     in1=bias_sum[:, k - 1, cols], op0=ALU.mult, op1=ALU.add))
            dve.wait_ge(s_pool0, 2)
            then_wait(v.tensor_scalar(w_clamp, w_all, SMALLEST_SCALE, None, ALU.max))
            then_wait(v.tensor_scalar(h_scale.bitcast(U32), w_clamp.bitcast(U32), EXPONENT_BITS, None, ALU.bitwise_and))
            then_wait(v.tensor_scalar(h_scale2, h_scale, 2.0, None, ALU.mult))
            v.tensor_scalar(neg_h_scale[:], h_scale, -2.0, None, ALU.mult).then_inc(s_ready, 1)
            then_wait(v.reciprocal(w_scale, h_scale2))
            part = w_h[:].rearrange("p s a b c -> p s (a b c)")
            then_wait(v.tensor_scalar(part[:, 0], flat, w_scale, None, ALU.mult))
            then_wait(v.scalar_tensor_tensor(out=part[:, 1], in0=flat, scalar=w_scale, in1=part[:, 0],
                                             op0=ALU.mult, op1=ALU.subtract))
            then_wait(v.tensor_scalar(w_o[:], w_o_in[:], w_scale, None, ALU.mult))
            v.memset(h32[:], 0.0).then_inc(g["h"], 1)
            for t_, s_ in ((u_a, "u_a"), (u_b, "u_b"), (h_a, "h_a"), (h_b, "h_b")):
                v.memset(t_[:], 0.0).then_inc(g[s_], 1)
            v.memset(ones16[:], 1.0).then_inc(s_ready, 1)
            dve.wait_ge(s_ready, 8)

            def masked(i, at):
                q = i % 2
                dve.wait_ge(front["gate"], at(1))
                dve.wait_ge(f_emb[q], landed(dve, i, at))
                wait(dve, front["xm"], at(0))
                for j in range(T):
                    last = v.tensor_scalar(mask[:, j], unit, gate[:, q, j:j + 1], frac[:, q, j:j + 1], ALU.is_lt, ALU.add)
                last.then_inc(front["mask"], 1)
                dve.wait_ge(front["mask"], at(1))
                wait(dve, front["xm_t"], at(0))
                v.tensor_tensor(xm[:], mask[:], emb[:, q, :, 0:D], ALU.mult).then_inc(front["xm"], 1)

            def residual(i, at):
                q = i % 2
                dve.wait_ge(front["att"], at(1))
                sums = [o_bank[k][:, 0:2 * ROW].rearrange("p (t d) -> p t d", t=2) for k in range(2)]
                wait(dve, front["h2"], at(0))
                v.reciprocal(rsum[:, 0:2], sums[0][:, :, D])
                v.reciprocal(rsum[:, 2:4], sums[1][:, :, D]).then_inc(front["rsum"], 1)
                dve.wait_ge(front["rsum"], at(1))
                wait(dve, f_store[q], stored(dve, i, at))
                for j in range(T):
                    last = v.scalar_tensor_tensor(out=h2[:, q, j], in0=sums[j // 2][:, j % 2, 0:D], scalar=rsum[:, j:j + 1],
                                                  in1=h1[:, q, j], op0=ALU.mult, op1=ALU.add)
                last.then_inc(front["h2"], 1)
                dve.wait_ge(front["h2"], at(1))
                statistics(i, at, h2[:, q], stat2, mv2, var2, "2")

            def statistics(i, at, src, stat, mv, var, which):
                for j in range(T):
                    last = v.bn_stats(stat[:, j], src[:, j])
                last.then_inc(front["bn" + which], 1)
                wait_apart(dve, front["bn" + which], at(1), s_ready, 8)
                for j in range(T):
                    last = v.bn_aggr(mv[:, j], stat[:, j])
                last.then_inc(front["mv" + which], 1)
                dve.wait_ge(front["mv" + which], at(1))
                wait(dve, front["rstd" + which], at(0))
                v.tensor_scalar(var[:], mv[:, :, 1], EPS, None, ALU.add).then_inc(front["var" + which], 1)

            def normalise(i, at, dst, src, mv, rstd, which, s):
                dve.wait_ge(front["rstd" + which], at(1))
                for j in range(T):
                    last = v.tensor_scalar(dst[:, j, 0:D], src[:, j], mv[:, j, 0:1], rstd[:, j:j + 1], ALU.subtract, ALU.mult)
                last.then_inc(front[s], 1)

            def experts(i, at):
                dve.wait_ge(front["gate_t"], at(1))
                dve.wait_ge(front["xmT"], at(1))
                wait(dve, front["y"], at(0))
                v.tensor_scalar(bias_row[:], gT[:], row_from, None, ALU.is_gt).then_inc(front["bias_row"], 1)
                for e in range(1, E):
                    last = v.scalar_tensor_tensor(out=kept[:, e - 1], in0=gT[:], scalar=EXPERT_FROM[e], in1=xmT[:],
                                                  op0=ALU.is_gt, op1=ALU.mult)
                last.then_inc(front["kept"], 1)

            def stages(i, at):
                nxt = lambda k: at(k + 1)
                prev = lambda k: at(k - 1)
                if i + 1 < B:
                    masked(i + 1, nxt)
                if 1 <= i:
                    residual(i - 1, prev)
                if i + 1 < B:
                    experts(i + 1, nxt)
                if 1 <= i:
                    wait(dve, front["xf_t"], prev(0))
                    normalise(i - 1, prev, xf[:], h2[:, (i - 1) % 2], mv2, rstd2, "2", "xf")
                if i + 1 < B:
                    dve.wait_ge(front["h1"], nxt(1))
                    statistics(i + 1, nxt, h1[:, (i + 1) % 2], stat1, mv1, var1, "1")
                    if i >= 1:
                        dve.wait_ge(front["att"], at(0))
                    normalise(i + 1, nxt, xn[:, (i + 1) % 2], h1[:, (i + 1) % 2], mv1, rstd1, "1", "xn")

            front_schedule(dve, stages)

            def scan(at, group, load, first):
                for s in range(BODY):
                    q = s // GS
                    now, nxt = at(s + 1), at(s + 2)
                    old = h32[:, :, (s - 1) % BODY * B:(s - 1) % BODY * B + B]
                    new = h32[:, :, s * B:s * B + B]
                    dve.wait_ge(g["r"], now)
                    v.tensor_tensor(rh_a[:], r[:], old, ALU.mult).then_inc(g["rh_a"], 1)
                    v.tensor_tensor(rh[:], r[:], old, ALU.mult).then_inc(g["rh"], 1)
                    dve.wait_ge(g["rh"], now)
                    v.tensor_tensor(rh_b[:], rh[:], rh_a[:], ALU.subtract).then_inc(g["rh_b"], 1)
                    dve.wait_ge(g["z"], now)
                    v.tensor_tensor(zh_a[:], z[:], old, ALU.mult).then_inc(g["zh_a"], 1)
                    v.tensor_tensor(zh[:], z[:], old, ALU.mult).then_inc(g["zh"], 1)
                    dve.wait_ge(g["zh"], now)
                    v.tensor_tensor(zh_b[:], zh[:], zh_a[:], ALU.subtract).then_inc(g["zh_b"], 1)
                    dve.wait_ge(g["c"], now)
                    v.tensor_tensor(u_a[:], c[:], omz[:], ALU.mult).then_inc(g["u_a"], 1)
                    v.tensor_tensor(u[:], c[:], omz[:], ALU.mult).then_inc(g["u"], 1)
                    dve.wait_ge(g["u"], now)
                    v.tensor_tensor(u_b[:], u[:], u_a[:], ALU.subtract).then_inc(g["u_b"], 1)
                    v.tensor_tensor(new, u[:], zh[:], ALU.add).then_inc(g["h"], 1)
                    v.tensor_tensor(h_a[:], u[:], zh[:], ALU.add).then_inc(g["h_a"], 1)
                    dve.wait_ge(g["h_a"], nxt)
                    v.tensor_tensor(h_b[:], new, h_a[:], ALU.subtract).then_inc(g["h_b"], 1)

            scan_schedule(dve, scan)

        @block.tensor
        def _(pe):
            mm = nc.tensor.matmul
            pe.wait_ge(s_ready, 8)
            pe.wait_ge(s_small, 16)

            def transposes(dst, src, s):
                for j in range(T):
                    last = nc.tensor.transpose(dst[:, j * P:(j + 1) * P], src(j), ident)
                last.then_inc(s, 1)

            def stages(i, at):
                q = i % 2
                if 0 <= i < B:
                    pe.wait_ge(front["xn"], at(1))
                    wait(pe, front["scan_x"], at(-1))
                    transposes(misc, lambda j: xn[:, q, j, 0:D], front["xn_t"])
                if i + 1 < B:
                    pe.wait_ge(front["xm"], at(2))
                    wait(pe, front["xmT"], at(1))
                    transposes(tT, lambda j: xm[:, j], front["xm_t"])
                    wait(pe, front["kept"], at(1))
                    transposes(gT, lambda j: gate[:, 1 - q, j:j + 1].to_broadcast([P, P]), front["gate_t"])
                if 0 <= i < B:
                    pe.wait_ge(front["xnT"], at(1))
                    wait(pe, f_tanh[T - 1], at(0))
                    mm(sc[1][:], w_attn[:], xnT[:], start=True, stop=True).then_inc(front["proj"], 1)
                    pe.wait_ge(front["projT"], at(1))
                    for t in range(T):
                        if t >= 2:
                            pe.wait_ge(f_tanh[t - 2], at(1))
                        else:
                            wait(pe, f_tanh[t + 2], at(0))
                        mm(sc[t % 2][:], xnT[:, t * P:(t + 1) * P], projT[:], start=True, stop=True).then_inc(f_score[t], 1)
                if 1 <= i:
                    pe.wait_ge(front["xf"], at(0))
                    if i < B:
                        pe.wait_ge(front["xnT"], at(1))
                    else:
                        pe.wait_ge(front["scan_x"], at(-1))
                    transposes(misc, lambda j: xf[:, j], front["xf_t"])
                if i + 1 < B:
                    pe.wait_ge(front["xmT"], at(2))
                    pe.wait_ge(front["bias_row"], at(2))
                    wait(pe, front["h1"], at(1))
                    for j in range(T):
                        cols = slice(j * P, (j + 1) * P)
                        mm(y_bank[:, cols], xmT[:, cols], w_expert[:, 0], start=True, stop=False)
                        mm(y_bank[:, cols], bias_row[:, cols], bias_e, start=False, stop=False)
                        if j == 0:
                            pe.wait_ge(front["kept"], at(2))
                        for e in range(1, E):
                            last = mm(y_bank[:, cols], kept[:, e - 1, cols], w_expert[:, e], start=False, stop=(e == E - 1))
                    last.then_inc(front["y"], 1)
                if 0 <= i < B:
                    wait(pe, front["h2"], at(0))
                    for j in range(T):
                        dst = o_bank[j // 2][:, j % 2 * ROW:j % 2 * ROW + ROW]
                        for t in range(T):
                            if j == 0:
                                pe.wait_ge(f_exp[t], at(1))
                            last = mm(dst, ex[:, t, j * P:(j + 1) * P], xn[:, q, t, :], start=(t == 0), stop=(t == T - 1))
                    last.then_inc(front["att"], 1)

            front_schedule(pe, stages)
            pe.wait_ge(front["scan_x"], B)

            def acc(dst, w, x, first=False, last=False):
                return mm(dst, w, x, start=first, stop=last, skip_group_check=True)

            def project(gate_n, m, pre, cols):
                units = slice(m * P, (m + 1) * P)
                acc(pre[:, m, :], w_x[:, gate_n, units], scan_x[:, cols], first=(m == 0))
                acc(pre[:, m, :], bias_x[:, gate_n * H + m * P:gate_n * H + (m + 1) * P], ones16[:], last=True)

            def recur(gate_n, pre, k, x):
                for m in range(KC):
                    for c_ in range(KC):
                        for part_ in range(2):
                            last = acc(pre[:, m, k:k + B], w_h[:, part_, gate_n, c_, m * P:(m + 1) * P], x[:, c_, :], last=True)
                return last

            Z, R, C = 0, 1, 2
            for gate_n, pre in ((R, pre_r), (Z, pre_z), (C, pre_c)):
                for m in range(KC):
                    project(gate_n, m, pre[0], slice(0, GC))

            def out_product(o, half, hist):
                acc(pre_o[o], h32[:, hist, o * GC:(o + 1) * GC], w_o[:, hist, :], first=(hist == 0))
                if half == 1:
                    return acc(pre_o[o], ones16[:], bias_o, last=True)

            def scan(at, group, load, first):
                for s in range(BODY):
                    q, k = s // GS, s % GS
                    o, cols = 1 - q, slice(k * B, k * B + B)
                    now = at(s + 1)
                    if k == 0:
                        ahead = at(GS * (q + 1))
                        cols_ahead = slice(ahead * B, ahead * B + GC) if isinstance(ahead, int) else \
                            bass.ds(pe.snap(ahead * B), GC)

                    def side(second):
                        if k == 0:
                            if first and q == 0:
                                return
                            if not second:
                                wait(pe, g["o_sig"], group(q - 2))
                                pe.wait_ge(g["h"], now)
                                out_product(o, 0, 0)
                            else:
                                out_product(o, 1, 1).then_inc(g["o_pre"], 1)
                        else:
                            gate_n, pre = ((R, pre_r), (Z, pre_z), (C, pre_c))[k - 1]
                            project(gate_n, 1 if second else 0, pre[1 - q], cols_ahead)

                    pe.wait_ge(g["u_a"], now)
                    recur(R, pre_r[q], k * B, u_a)
                    pe.wait_ge(g["u_b"], now)
                    recur(R, pre_r[q], k * B, u_b).then_inc(g["r_pre"], 1)
                    pe.wait_ge(g["h_a"], now)
                    recur(Z, pre_z[q], k * B, h_a)
                    pe.wait_ge(g["h_b"], now)
                    recur(Z, pre_z[q], k * B, h_b).then_inc(g["z_pre"], 1)
                    side(False)
                    pe.wait_ge(g["rh_a"], now)
                    recur(C, pre_c[q], k * B, rh_a)
                    pe.wait_ge(g["rh_b"], now)
                    recur(C, pre_c[q], k * B, rh_b).then_inc(g["c_pre"], 1)
                    side(True)
                    q2, k2 = (s + 1) % BODY // GS, (s + 1) % GS * B
                    pe.wait_ge(g["zh_a"], now)
                    recur(R, pre_r[q2], k2, zh_a)
                    pe.wait_ge(g["zh_b"], now)
                    recur(R, pre_r[q2], k2, zh_b)

            scan_schedule(pe, scan)
            wait(pe, g["o_sig"], S // GS - 2)
            pe.wait_ge(g["h"], S + 1)
            out_product(1, 0, 0)
            out_product(1, 1, 1).then_inc(g["o_pre"], 1)


def kernel(**inputs):
    import numpy as np
    import concourse.bacc as bacc
    from concourse.bass_utils import run_bass_kernel_spmd

    a = {k: np.asarray(v) for k, v in inputs.items()}
    f = {k.removeprefix("L0_ffn_"): v for k, v in a.items() if k.startswith("L0_ffn_")}

    def partitions(w):
        return w.reshape(-1, P, w.shape[1]).transpose(1, 0, 2)

    row = np.arange(P)
    consts = np.zeros((P, 2 * P + 7), np.float32)
    consts[:, 0:P] = np.eye(P)
    consts[:, P:2 * P] = row[None, :]
    rows_of_parts = row < 3 * E
    consts[:, 2 * P] = np.where(rows_of_parts, np.where(row % E == 0, -3e38, (D // E) * (row % E) - 1), 3e38)
    for i in range(3):
        consts[:, 2 * P + 1 + i] = rows_of_parts & (row // E == i)
        consts[:, 2 * P + 4 + i] = row == i

    arrays = {
        "x_cols": a["x"].reshape(B * T, P).T,
        "table": np.concatenate([a["L0_tok_emb_table"], a["L0_tok_gate_table"]], axis=1),
        "expert_wT": a["L0_tok_expert_w"].transpose(2, 0, 1),
        "expert_b": a["L0_tok_expert_b"],
        "attn_w": a["L0_attn_attention_weights"],
        "wxT": np.stack([f[n].T for n in ("Wuz", "Wur", "Wu")], axis=1),
        "bx": np.concatenate([f["buz"], f["bur"], f["bu"]])[None],
        "bh": np.concatenate([f["bwz"], f["bwr"], f["bw"]])[None],
        "whT": np.stack([partitions(f[n].T) for n in ("Wwz", "Wwr", "Ww")], axis=1),
        "woT": partitions(f["Wo"].T),
        "bo": f["bo"][None],
        "consts": consts,
    }
    arrays = {k: np.ascontiguousarray(v) for k, v in arrays.items()}
    nc = bacc.Bacc("TRN2", target_bir_lowering=False, num_devices=1)
    args = [nc.dram_tensor(k, v.shape, mybir.dt.from_np(v.dtype), kind="ExternalInput").ap() for k, v in arrays.items()]
    out = nc.dram_tensor("out", (B, S, D), F32, kind="ExternalOutput").ap()
    tower_kernel(nc, *args, out)
    return run_bass_kernel_spmd(nc, [arrays], core_ids=[0]).results[0]["out"]
```

```python
from contextlib import ExitStack

import concourse.bass as bass
from concourse import mybir

F32 = mybir.dt.float32
F16 = mybir.dt.float16
BF16 = mybir.dt.bfloat16
I32 = mybir.dt.int32
U32 = mybir.dt.uint32
ALU = mybir.AluOpType
ACT = mybir.ActivationFunctionType
AX_X = mybir.AxisListType.X
RMAX = bass.bass_isa.ReduceOp.max

P = 128
B, S, D, H, E = 32, 512, 128, 256, 5
T = S // P
ROW = D + 1
KC = H // P
GS = 4
GC = GS * B
BODY = 2 * GS
BIG = float(2 ** 23)
L_CONST = 1e9
EXPERT_SPAN = D // E
EXPERT_FROM = [float(EXPERT_SPAN * e - 1) for e in range(E)]
EPS = 1e-5
SMALLEST_SCALE = 2.0 ** -12
EXPONENT_BITS = 0x7F800000


def tower_kernel(nc, x_cols, table, expert_wT, expert_b, attn_w, wxT, bx, bh, whT, woT, bo, consts, out):
    h2_dram = nc.dram_tensor("residual_scratch", (B, S, D), F32, kind="Internal").ap()

    with ExitStack() as ctx:
        def sb(name, shape, dt=F32):
            return ctx.enter_context(nc.sbuf_tensor(name, shape, dt))

        def sem(name):
            return ctx.enter_context(nc.semaphore(name))

        bank = [ctx.enter_context(nc.psum_tensor(f"bank{i}", [P, 512], F32)) for i in range(8)]

        const = sb("const", [P, 2 * P + 7])
        ident, unit = const[:, 0:P], const[:, P:2 * P]
        row_from = const[:, 2 * P:2 * P + 1]
        exp_part = [const[:, 2 * P + 1 + i:2 * P + 2 + i] for i in range(3)]
        one_part = [const[:, 2 * P + 4 + i:2 * P + 5 + i] for i in range(3)]
        ones16 = sb("ones16", [P, P], BF16)
        token_id = sb("token_id", [P, B * T], I32)
        w_expert = sb("w_expert", [P, E, D])
        w_expert_in = sb("w_expert_in", [P, E, D])
        w_attn = sb("w_attn", [P, D])
        w_x = sb("w_x", [P, 3, H])
        w_h_in = sb("w_h_in", [P, 3, KC, H])
        w_h = sb("w_h", [P, 2, 3, KC, H], F16)
        w_o_in = sb("w_o_in", [P, KC, D])
        w_o = sb("w_o", [P, KC, D])
        NBIAS = 3 * H + 2 * D
        bias_in = sb("bias_in", [P, NBIAS])
        bias_less = sb("bias_less", [P, NBIAS])
        bias_rest = sb("bias_rest", [P, 3, NBIAS])
        bias_part = sb("bias_part", [P, 3, NBIAS], BF16)
        bias_sum = sb("bias_sum", [P, 3, NBIAS], BF16)
        bias_x, bias_o = bias_sum[:, 2, 0:3 * H], bias_sum[:, 2, 3 * H:3 * H + D]
        bias_e = bias_sum[:, 2, 3 * H + D:NBIAS]
        scales = sb("scales", [P, 8])
        w_max, w_min, w_abs, w_all, w_clamp, h_scale, h_scale2, w_scale = (scales[:, i:i + 1] for i in range(8))
        neg_h_scale = sb("neg_h_scale", [P, 1])

        ids_now = sb("ids_now", [P, 2, T], I32)
        emb = sb("emb", [P, 2, T, ROW])
        gate = sb("gate", [P, 2, T])
        frac = sb("frac", [P, 2, T])
        gwork = sb("gwork", [P, 8, T])
        mask = sb("mask", [P, T, P])
        xm = sb("xm", [P, T, P])
        xmT = sb("xmT", [P, T * P])
        kept = sb("kept", [P, E - 1, T * P])
        bias_row = sb("bias_row", [P, T * P], BF16)
        h1 = sb("h1", [P, 2, T, P])
        stat1, stat2 = sb("stat1", [P, T, 6]), sb("stat2", [P, T, 6])
        mv1, mv2 = sb("mv1", [P, T, 2]), sb("mv2", [P, T, 2])
        var1, var2 = sb("var1", [P, T]), sb("var2", [P, T])
        rstd1, rstd2 = sb("rstd1", [P, T]), sb("rstd2", [P, T])
        minus_half = sb("minus_half", [P, T])
        xn = sb("xn", [P, 2, T, ROW])
        xnT = sb("xnT", [P, T * P])
        projT = sb("projT", [P, T * P])
        th = sb("th", [P, T, T * P])
        ex = sb("ex", [P, T, T * P])
        rsum = sb("rsum", [P, T])
        h2 = sb("h2", [P, 2, T, P])
        xf = sb("xf", [P, T, P])
        scan_x = sb("scan_x", [P, (S + GS) * B])

        h32 = sb("h32", [P, KC, BODY * B])
        h_a, h_b = sb("h_a", [P, KC, B], F16), sb("h_b", [P, KC, B], F16)
        r, z, c = sb("r", [P, KC, B]), sb("z", [P, KC, B]), sb("c", [P, KC, B])
        rh, rh_a, rh_b = sb("rh", [P, KC, B]), sb("rh_a", [P, KC, B], F16), sb("rh_b", [P, KC, B], F16)
        zh, zh_a, zh_b = sb("zh", [P, KC, B]), sb("zh_a", [P, KC, B], F16), sb("zh_b", [P, KC, B], F16)
        omz = sb("omz", [P, KC, B])
        u, u_a, u_b = sb("u", [P, KC, B]), sb("u_a", [P, KC, B], F16), sb("u_b", [P, KC, B], F16)
        res = sb("res", [P, 2, D])
        sig = sb("sig", [P, 2, D])
        fin = sb("fin", [P, 2, D])

        s_ids, s_in, s_wh = sem("s_ids"), sem("s_in"), sem("s_wh")
        s_bias_e, s_bias = sem("s_bias_e"), sem("s_bias")
        s_zero, s_dve, s_pool0 = sem("s_zero"), sem("s_dve"), sem("s_pool0")
        s_front, s_max, s_scan = sem("s_front"), sem("s_max"), sem("s_scan")
        front = {n: sem("f_" + n) for n in (
            "ids", "gate0", "gate", "mask", "xm", "xm_t", "gate_t", "xmT", "kept", "bias_row", "y", "h1", "bn1",
            "mv1", "var1", "rstd1", "xn", "xn_t", "xnT", "proj", "projT", "att", "rsum", "h2", "bn2", "mv2", "var2",
            "rstd2", "xf", "xf_t", "scan_x")}
        f_emb = [sem(f"f_emb{i}") for i in range(2)]
        f_store = [sem(f"f_store{i}") for i in range(2)]
        f_score = [sem(f"f_score{t}") for t in range(T)]
        f_tanh = [sem(f"f_tanh{t}") for t in range(T)]
        f_exp = [sem(f"f_exp{t}") for t in range(T)]
        g = {n: sem("g_" + n) for n in (
            "r_pre", "z_pre", "c_pre", "r", "z", "c", "rh", "rh_a", "rh_b", "zh", "zh_a", "zh_b", "omz",
            "u", "u_a", "u_b", "h", "h_a", "h_b", "o_pre", "o_sig", "o_fin")}
        o_res = [sem(f"o_res{i}") for i in range(2)]
        o_store = [sem(f"o_store{i}") for i in range(2)]

        tT, gT, sc, y_bank, o_bank, misc = bank[0], bank[1], bank[2:4], bank[4], bank[5:7], bank[7]
        pre_r = [bank[i][:, 0:KC * GC].rearrange("p (m n) -> p m n", m=KC) for i in (0, 1)]
        pre_z = [bank[i][:, 0:KC * GC].rearrange("p (m n) -> p m n", m=KC) for i in (2, 3)]
        pre_c = [bank[i][:, 0:KC * GC].rearrange("p (m n) -> p m n", m=KC) for i in (4, 5)]
        pre_o = [bank[i][:, 0:D] for i in (6, 7)]

        def rows(eng, base):
            if isinstance(base, int):
                return lambda k: base + k
            cache = {}

            def at(k):
                if k not in cache:
                    cache[k] = eng.snap(base + k)
                return cache[k]
            return at

        def wait(eng, s, value):
            if not (isinstance(value, int) and value <= 0):
                eng.wait_ge(s, value)

        def wait_apart(eng, s, value, constants, count):
            if not isinstance(value, int):
                value = eng.to_reg(value)
            eng.wait_ge(constants, count)
            wait(eng, s, value)

        def landed(eng, i, at):
            base = at(0)
            if isinstance(base, int):
                return 16 * T * (base // 2 + 1)
            return eng.snap((base - i % 2) * (8 * T) + 16 * T)

        def gate_steps(eng, at, per_row, k):
            base = at(0)
            return base * per_row + k if isinstance(base, int) else eng.snap(base * per_row + k)

        def stored(eng, i, at):
            base = at(0)
            if isinstance(base, int):
                return 16 * (base // 2)
            return eng.snap((base - i % 2) * 8)

        def front_schedule(eng, stages, scan_constants={}):
            for i in range(-3, 4):
                stages(i, rows(eng, i))
                if i in scan_constants:
                    scan_constants[i]()
            with eng.Fori(2, B // 2 - 2) as n:
                for p in range(2):
                    at = rows(eng, eng.snap(n * 2 + p))
                    stages(4 + p, at)
            for i in range(B - 4, B + 1):
                stages(i, rows(eng, i))
                if i in scan_constants:
                    scan_constants[i]()

        def is_row(i):
            return 0 <= i < B

        def scan_schedule(eng, body):
            for n in range(2):
                body(rows(eng, n * BODY), rows(eng, n * 2), rows(eng, n * 16), n == 0)
            with eng.Fori(2, S // BODY) as n:
                body(rows(eng, eng.snap(n * BODY)), rows(eng, eng.snap(n * 2)), rows(eng, eng.snap(n * 16)), False)

        block = ctx.enter_context(nc.Block())

        @block.sync
        def _(sp):
            sp.dma_start(token_id[:], x_cols).then_inc(s_ids, 16)
            sp.dma_start(const[:], consts).then_inc(s_in, 16)
            sp.dma_start(w_expert_in[:], expert_wT).then_inc(s_in, 16)
            sp.dma_start(w_attn[:], attn_w).then_inc(s_in, 16)
            sp.wait_ge(s_zero, 2)
            xo = slice(3 * H, 3 * H + D)
            xe = slice(3 * H + D, NBIAS)
            for i in range(3):
                sp.dma_start(bias_in[E * i:E * i + E, xe], expert_b).then_inc(s_bias_e, 16)
                sp.dma_start(bias_less[E * i + 1:E * i + E, xe], expert_b[0:E - 1, :]).then_inc(s_bias_e, 16)
            for i in range(3):
                sp.dma_start(bias_in[i:i + 1, 0:3 * H], bx).then_inc(s_bias, 16)
                sp.dma_start(bias_less[i:i + 1, 0:3 * H], bh).then_inc(s_bias, 16)
                sp.dma_start(bias_in[i:i + 1, xo], bo).then_inc(s_bias, 16)
            sp.dma_start(w_x[:], wxT).then_inc(s_wh, 16)
            sp.dma_start(w_h_in[:], whT).then_inc(s_wh, 16)
            sp.dma_start(w_o_in[:], woT).then_inc(s_wh, 16)

            def store_residual(i, at):
                if 0 <= i < B:
                    sp.wait_ge(front["h2"], at(1))
                    dst = h2_dram[bass.ds(at(0), 1), :, :].rearrange("b (j p) d -> p (b j) d", p=P)
                    sp.dma_start(dst, h2[:, i % 2]).then_inc(f_store[i % 2], 16)

            front_schedule(sp, store_residual)
            for i in range(2):
                sp.wait_ge(f_store[i], 16 * (B // 2))

            def rows_of(dram, at, q):
                return dram.rearrange("b s d -> s b d")[bass.ds(at(GS * q), GS), :, :]

            def results(at, group, load, first):
                for q in range(2):
                    if not first:
                        sp.wait_ge(g["o_fin"], group(q - 1))
                        sp.dma_start(rows_before(out, at, q), fin[:, q]).then_inc(o_store[q], 16)
                    sp.dma_start(res[:, q], rows_of(h2_dram, at, q)).then_inc(o_res[q], 16)

            def rows_before(dram, at, q):
                return dram.rearrange("b s d -> s b d")[bass.ds(at(GS * q - BODY), GS), :, :]

            scan_schedule(sp, results)
            for q in range(2):
                sp.wait_ge(g["o_fin"], S // GS - 1 + q)
                sp.dma_start(rows_of(out, lambda k: S - BODY + k, q), fin[:, q]).then_inc(o_store[q], 16)
            for q in range(2):
                sp.wait_ge(o_store[q], 16 * (S // BODY))

        @block.gpsimd
        def _(pool):
            nc.gpsimd.memset(minus_half[:], -0.5).then_inc(s_pool0, 1)
            pool.wait_ge(s_ids, 16)

            def pick_ids(i, at):
                q = i % 2
                nc.gpsimd.tensor_copy(ids_now[:, q], token_id[:, bass.ds(at(0) * T, T)]).then_inc(front["ids"], 1)
                wait_apart(pool, front["ids"], at(1), s_pool0, 1)
                wait(pool, front["xm"], at(-1))

            def gather(i, tiles):
                q = i % 2
                for j in tiles:
                    sent = nc.gpsimd.indirect_dma_start(
                        out=emb[:, q, j, :], out_offset=None, in_=table,
                        in_offset=bass.IndirectOffsetOnAxis(ap=ids_now[:, q, j:j + 1].bitcast(U32), axis=0))
                    sent.then_inc(f_emb[q], 16)

            chain = [0]

            def gates(i, at):
                q = i % 2
                lands = landed(pool, i, at)
                row_before = at(-1) if isinstance(at(-1), int) else pool.to_reg(at(-1))
                wait_apart(pool, f_emb[q], lands, s_pool0, 1)
                wait(pool, front["gate_t"], row_before)
                ts, tt, w = nc.gpsimd.tensor_scalar, nc.gpsimd.tensor_tensor, gwork
                steps = [
                    lambda: ts(gate[:, q], emb[:, q, :, D], float(D), None, ALU.mult),
                    lambda: ts(w[:, 0], gate[:, q], L_CONST, BIG, ALU.mult, ALU.min),
                    lambda: ts(w[:, 1], w[:, 0], -BIG, None, ALU.max),
                    lambda: ts(w[:, 2], w[:, 1], 0.0, BIG, ALU.max, ALU.add),
                    lambda: ts(w[:, 3], w[:, 1], 0.0, -BIG, ALU.min, ALU.add),
                    lambda: ts(w[:, 3], w[:, 3], BIG, None, ALU.add),
                    lambda: ts(w[:, 2], w[:, 2], -BIG, None, ALU.add),
                    lambda: tt(w[:, 4], w[:, 2], w[:, 3], ALU.add),
                    lambda: tt(w[:, 5], w[:, 4], w[:, 1], ALU.subtract),
                    lambda: ts(w[:, 6], w[:, 5], 0.0, None, ALU.is_gt),
                    lambda: tt(w[:, 7], w[:, 6], w[:, 5], ALU.subtract),
                    lambda: ts(frac[:, q], w[:, 7], 1.0 / L_CONST, None, ALU.mult),
                ]
                for k, step in enumerate(steps):
                    step().then_inc(front["gate0"] if k < len(steps) - 1 else front["gate"], 1)
                    if k < len(steps) - 1:
                        wait_apart(pool, front["gate0"], gate_steps(pool, at, len(steps) - 1, k + 1), s_pool0, 1)

            def power(i, at, var, rstd, which, reader):
                pool.wait_ge(front["var" + which], at(1))
                wait(pool, front[reader], at(0))
                nc.gpsimd.tensor_tensor(rstd[:], var[:], minus_half[:], ALU.pow).then_inc(front["rstd" + which], 1)

            def stages(i, at):
                if is_row(i + 2):
                    gates(i + 2, lambda k: at(k + 2))
                if is_row(i + 3):
                    pick_ids(i + 3, lambda k: at(k + 3))
                    gather(i + 3, (0, 1))
                if is_row(i - 1):
                    power(i - 1, lambda k: at(k - 1), var2, rstd2, "2", "xf")
                if is_row(i + 3):
                    gather(i + 3, (2, 3))
                if is_row(i + 1):
                    power(i + 1, lambda k: at(k + 1), var1, rstd1, "1", "xn")

            pool.wait_ge(s_pool0, 1)

            def largest():
                pool.wait_ge(s_max, 3)
                nc.gpsimd.partition_all_reduce(w_all, w_abs, P, RMAX).then_inc(s_max, 1)

            front_schedule(pool, stages, {B - 2: largest})

            def results(at, group, load, first):
                for q in range(2):
                    if not (first and q == 0):
                        output(group(q), load, q)

            def output(count, load, q):
                o = 1 - q
                pool.wait_ge(g["o_sig"], count)
                pool.wait_ge(o_res[o], load(16 if o == 0 else 0))
                wait(pool, o_store[o], load(0 if o == 0 else -16))
                nc.gpsimd.tensor_tensor(fin[:, o], sig[:, o], res[:, o], ALU.add).then_inc(g["o_fin"], 1)

            scan_schedule(pool, results)
            output(S // GS, lambda k: 16 * (S // BODY) + k, 0)

        @block.scalar
        def _(act):
            def copy(dst, src, s):
                nc.scalar.copy(dst, src).then_inc(s, 1)

            def stages(i, at):
                if is_row(i):
                    act.wait_ge(front["xn_t"], at(1))
                    copy(xnT[:], misc[:], front["xnT"])
                    act.wait_ge(front["proj"], at(1))
                    copy(projT[:], sc[1][:], front["projT"])
                if is_row(i + 1):
                    act.wait_ge(front["y"], at(2))
                    if i >= 1:
                        act.wait_ge(front["h2"], at(0))
                    copy(h1[:, (i + 1) % 2].rearrange("p t d -> p (t d)"), y_bank[:], front["h1"])
                if is_row(i + 2):
                    act.wait_ge(front["xm_t"], at(3))
                    wait(act, front["y"], at(2))
                    copy(xmT[:], tT[:], front["xmT"])
                if is_row(i):
                    for t in range(T + 1):
                        if t < T:
                            act.wait_ge(f_score[t], at(1))
                            nc.scalar.activation(th[:, t], sc[t % 2][:], ACT.Tanh).then_inc(f_tanh[t], 1)
                        if t >= 1:
                            act.wait_ge(f_tanh[t - 1], at(1))
                            nc.scalar.activation(ex[:, t - 1], th[:, t - 1], ACT.Exp).then_inc(f_exp[t - 1], 1)
                if is_row(i - 1):
                    act.wait_ge(front["xf_t"], at(0))
                    dst = scan_x[:, 0:S * B].rearrange("p (s b) -> p s b", b=B)[:, :, bass.ds(at(-1), 1)]
                    copy(dst.rearrange("p s b -> p (s b)"), misc[:], front["scan_x"])

            front_schedule(act, stages)

            def scan(at, group, load, first):
                for s in range(BODY):
                    q, k = s // GS, s % GS * B
                    now = at(s + 1)
                    act.wait_ge(g["r_pre"], now)
                    nc.scalar.activation(r[:], pre_r[q][:, :, k:k + B], ACT.Sigmoid).then_inc(g["r"], 1)
                    act.wait_ge(g["z_pre"], now)
                    nc.scalar.activation(z[:], pre_z[q][:, :, k:k + B], ACT.Sigmoid).then_inc(g["z"], 1)
                    act.wait_ge(g["z"], now)
                    nc.scalar.activation(omz[:], z[:], ACT.Identity, scale=neg_h_scale[:], bias=h_scale2).then_inc(g["omz"], 1)
                    act.wait_ge(g["c_pre"], now)
                    nc.scalar.activation(c[:], pre_c[q][:, :, k:k + B], ACT.Tanh).then_inc(g["c"], 1)
                    if s % GS == 1 and not (first and q == 0):
                        output(group(q), group(q - 2), q)

            def output(count, used, q):
                o = 1 - q
                act.wait_ge(g["o_pre"], count)
                wait(act, g["o_fin"], used)
                nc.scalar.activation(sig[:, o], pre_o[o], ACT.Sigmoid).then_inc(g["o_sig"], 1)

            scan_schedule(act, scan)
            output(S // GS, S // GS - 2, 0)

        @block.vector
        def _(dve):
            v = nc.vector
            done = [0]

            def then_wait(ins):
                done[0] += 1
                ins.then_inc(s_dve, 1)
                dve.wait_ge(s_dve, done[0])

            v.memset(bias_in[:], 0.0).then_inc(s_zero, 1)
            v.memset(bias_less[:], 0.0).then_inc(s_zero, 1)
            v.memset(scan_x[:, S * B:], 0.0).then_inc(s_front, 1)
            v.memset(xn[:, :, :, D:ROW], 1.0).then_inc(s_front, 1)
            v.memset(ones16[:], 1.0).then_inc(s_front, 1)
            dve.wait_ge(s_in, 48)
            v.tensor_copy(w_expert[:, 0], w_expert_in[:, 0]).then_inc(s_front, 1)
            v.tensor_tensor(w_expert[:, 1:E], w_expert_in[:, 1:E], w_expert_in[:, 0:E - 1], ALU.subtract).then_inc(s_front, 1)

            def bias_rows(cols, pick, op):
                then_wait(v.tensor_tensor(bias_rest[:, 0, cols], bias_in[:, cols], bias_less[:, cols], op))
                for k in range(3):
                    then_wait(v.tensor_copy(bias_part[:, k, cols], bias_rest[:, k, cols]))
                    if k < 2:
                        then_wait(v.tensor_tensor(bias_rest[:, k + 1, cols], bias_rest[:, k, cols], bias_part[:, k, cols],
                                                  ALU.subtract))
                then_wait(v.tensor_scalar(bias_sum[:, 0, cols], bias_part[:, 0, cols], pick[0], None, ALU.mult))
                for k in (1, 2):
                    then_wait(v.scalar_tensor_tensor(out=bias_sum[:, k, cols], in0=bias_part[:, k, cols], scalar=pick[k],
                                                     in1=bias_sum[:, k - 1, cols], op0=ALU.mult, op1=ALU.add))

            dve.wait_ge(s_bias_e, 16 * 6)
            bias_rows(slice(3 * H + D, NBIAS), exp_part, ALU.subtract)

            flat = w_h_in[:].rearrange("p a b c -> p (a b c)")

            def gate_biases():
                dve.wait_ge(s_bias, 16 * 9)
                bias_rows(slice(0, 3 * H + D), one_part, ALU.add)

            def weight_magnitudes():
                dve.wait_ge(s_wh, 48)
                v.tensor_reduce(w_max, flat, AX_X, ALU.max).then_inc(s_max, 1)
                v.tensor_reduce(w_min, flat, AX_X, ALU.min).then_inc(s_max, 1)
                dve.wait_ge(s_max, 2)
                v.scalar_tensor_tensor(out=w_abs, in0=w_min, scalar=-1.0, in1=w_max, op0=ALU.mult, op1=ALU.max).then_inc(s_max, 1)
                v.memset(h32[:], 0.0).then_inc(g["h"], 1)
                for t_, s_ in ((u_a, "u_a"), (u_b, "u_b"), (h_a, "h_a"), (h_b, "h_b")):
                    v.memset(t_[:], 0.0).then_inc(g[s_], 1)

            def weight_parts():
                dve.wait_ge(s_max, 4)
                then_wait(v.tensor_scalar(w_clamp, w_all, SMALLEST_SCALE, None, ALU.max))
                then_wait(v.tensor_scalar(h_scale.bitcast(U32), w_clamp.bitcast(U32), EXPONENT_BITS, None, ALU.bitwise_and))
                then_wait(v.tensor_scalar(h_scale2, h_scale, 2.0, None, ALU.mult))
                then_wait(v.reciprocal(w_scale, h_scale2))
                v.tensor_scalar(neg_h_scale[:], h_scale, -2.0, None, ALU.mult).then_inc(s_scan, 1)
                part = w_h[:].rearrange("p s a b c -> p s (a b c)")
                then_wait(v.tensor_scalar(part[:, 0], flat, w_scale, None, ALU.mult))
                v.scalar_tensor_tensor(out=part[:, 1], in0=flat, scalar=w_scale, in1=part[:, 0],
                                       op0=ALU.mult, op1=ALU.subtract).then_inc(s_scan, 1)
                v.tensor_scalar(w_o[:], w_o_in[:], w_scale, None, ALU.mult).then_inc(s_scan, 1)

            def masked(i, at):
                q = i % 2
                dve.wait_ge(front["gate"], at(1))
                dve.wait_ge(f_emb[q], landed(dve, i, at))
                for j in range(T):
                    last = v.tensor_scalar(mask[:, j], unit, gate[:, q, j:j + 1], frac[:, q, j:j + 1], ALU.is_lt, ALU.add)
                last.then_inc(front["mask"], 1)
                dve.wait_ge(front["mask"], at(1))
                wait(dve, front["xm_t"], at(0))
                v.tensor_tensor(xm[:], mask[:], emb[:, q, :, 0:D], ALU.mult).then_inc(front["xm"], 1)

            def residual(i, at):
                q = i % 2
                dve.wait_ge(front["att"], at(1))
                sums = [o_bank[k][:, 0:2 * ROW].rearrange("p (t d) -> p t d", t=2) for k in range(2)]
                v.reciprocal(rsum[:, 0:2], sums[0][:, :, D])
                v.reciprocal(rsum[:, 2:4], sums[1][:, :, D]).then_inc(front["rsum"], 1)
                dve.wait_ge(front["rsum"], at(1))
                wait(dve, f_store[q], stored(dve, i, at))
                for j in range(T):
                    last = v.scalar_tensor_tensor(out=h2[:, q, j], in0=sums[j // 2][:, j % 2, 0:D], scalar=rsum[:, j:j + 1],
                                                  in1=h1[:, q, j], op0=ALU.mult, op1=ALU.add)
                last.then_inc(front["h2"], 1)
                dve.wait_ge(front["h2"], at(1))
                statistics(i, at, h2[:, q], stat2, mv2, var2, "2")

            def statistics(i, at, src, stat, mv, var, which):
                for j in range(T):
                    last = v.bn_stats(stat[:, j], src[:, j])
                last.then_inc(front["bn" + which], 1)
                wait_apart(dve, front["bn" + which], at(1), s_front, 5)
                for j in range(T):
                    last = v.bn_aggr(mv[:, j], stat[:, j])
                last.then_inc(front["mv" + which], 1)
                dve.wait_ge(front["mv" + which], at(1))
                wait(dve, front["rstd" + which], at(0))
                v.tensor_scalar(var[:], mv[:, :, 1], EPS, None, ALU.add).then_inc(front["var" + which], 1)

            def normalise(i, at, dst, src, mv, rstd, which, s):
                dve.wait_ge(front["rstd" + which], at(1))
                for j in range(T):
                    last = v.tensor_scalar(dst[:, j, 0:D], src[:, j], mv[:, j, 0:1], rstd[:, j:j + 1], ALU.subtract, ALU.mult)
                last.then_inc(front[s], 1)

            def experts(i, at):
                dve.wait_ge(front["gate_t"], at(1))
                dve.wait_ge(front["xmT"], at(1))
                wait(dve, front["y"], at(0))
                v.tensor_scalar(bias_row[:], gT[:], row_from, None, ALU.is_gt).then_inc(front["bias_row"], 1)
                for e in range(1, E):
                    last = v.scalar_tensor_tensor(out=kept[:, e - 1], in0=gT[:], scalar=EXPERT_FROM[e], in1=xmT[:],
                                                  op0=ALU.is_gt, op1=ALU.mult)
                last.then_inc(front["kept"], 1)

            def stages(i, at):
                nxt = lambda k: at(k + 1)
                prev = lambda k: at(k - 1)
                if is_row(i - 1):
                    residual(i - 1, prev)
                if is_row(i + 2):
                    masked(i + 2, lambda k: at(k + 2))
                if is_row(i - 1):
                    wait(dve, front["xf_t"], prev(0))
                    normalise(i - 1, prev, xf[:], h2[:, (i - 1) % 2], mv2, rstd2, "2", "xf")
                if is_row(i + 1):
                    dve.wait_ge(front["h1"], nxt(1))
                    statistics(i + 1, nxt, h1[:, (i + 1) % 2], stat1, mv1, var1, "1")
                    if i >= 1:
                        dve.wait_ge(front["att"], at(0))
                    normalise(i + 1, nxt, xn[:, (i + 1) % 2], h1[:, (i + 1) % 2], mv1, rstd1, "1", "xn")
                if is_row(i + 2):
                    experts(i + 2, lambda k: at(k + 2))

            front_schedule(dve, stages, {-1: gate_biases, B - 3: weight_magnitudes, B - 1: weight_parts})

            def scan(at, group, load, first):
                for s in range(BODY):
                    q = s // GS
                    now, nxt = at(s + 1), at(s + 2)
                    old = h32[:, :, (s - 1) % BODY * B:(s - 1) % BODY * B + B]
                    new = h32[:, :, s * B:s * B + B]
                    dve.wait_ge(g["r"], now)
                    v.tensor_tensor(rh_a[:], r[:], old, ALU.mult).then_inc(g["rh_a"], 1)
                    v.tensor_tensor(rh[:], r[:], old, ALU.mult).then_inc(g["rh"], 1)
                    dve.wait_ge(g["rh"], now)
                    v.tensor_tensor(rh_b[:], rh[:], rh_a[:], ALU.subtract).then_inc(g["rh_b"], 1)
                    dve.wait_ge(g["z"], now)
                    v.tensor_tensor(zh_a[:], z[:], old, ALU.mult).then_inc(g["zh_a"], 1)
                    v.tensor_tensor(zh[:], z[:], old, ALU.mult).then_inc(g["zh"], 1)
                    dve.wait_ge(g["zh"], now)
                    v.tensor_tensor(zh_b[:], zh[:], zh_a[:], ALU.subtract).then_inc(g["zh_b"], 1)
                    dve.wait_ge(g["c"], now)
                    v.tensor_tensor(u_a[:], c[:], omz[:], ALU.mult).then_inc(g["u_a"], 1)
                    v.tensor_tensor(u[:], c[:], omz[:], ALU.mult).then_inc(g["u"], 1)
                    dve.wait_ge(g["u"], now)
                    v.tensor_tensor(u_b[:], u[:], u_a[:], ALU.subtract).then_inc(g["u_b"], 1)
                    v.tensor_tensor(new, u[:], zh[:], ALU.add).then_inc(g["h"], 1)
                    v.tensor_tensor(h_a[:], u[:], zh[:], ALU.add).then_inc(g["h_a"], 1)
                    dve.wait_ge(g["h_a"], nxt)
                    v.tensor_tensor(h_b[:], new, h_a[:], ALU.subtract).then_inc(g["h_b"], 1)

            scan_schedule(dve, scan)

        @block.tensor
        def _(pe):
            mm = nc.tensor.matmul
            pe.wait_ge(s_front, 5)

            def transposes(dst, src, s):
                for j in range(T):
                    last = nc.tensor.transpose(dst[:, j * P:(j + 1) * P], src(j), ident)
                last.then_inc(s, 1)

            def stages(i, at):
                q = i % 2

                def experts(tiles):
                    if tiles[0] == 0:
                        pe.wait_ge(front["kept"], at(2))
                        wait(pe, front["h1"], at(1))
                    for j in tiles:
                        cols = slice(j * P, (j + 1) * P)
                        mm(y_bank[:, cols], xmT[:, cols], w_expert[:, 0], start=True, stop=False)
                        mm(y_bank[:, cols], bias_row[:, cols], bias_e, start=False, stop=False)
                        for e in range(1, E):
                            last = mm(y_bank[:, cols], kept[:, e - 1, cols], w_expert[:, e], start=False, stop=(e == E - 1))
                    if tiles[-1] == T - 1:
                        last.then_inc(front["y"], 1)

                if is_row(i):
                    pe.wait_ge(front["xn"], at(1))
                    wait(pe, front["scan_x"], at(-1))
                    transposes(misc, lambda j: xn[:, q, j, 0:D], front["xn_t"])
                if is_row(i + 1):
                    experts((0, 1))
                if is_row(i):
                    pe.wait_ge(front["xnT"], at(1))
                    wait(pe, f_tanh[T - 1], at(0))
                    mm(sc[1][:], w_attn[:], xnT[:], start=True, stop=True).then_inc(front["proj"], 1)
                if is_row(i + 1):
                    experts((2, 3))
                if is_row(i + 2):
                    pe.wait_ge(front["xm"], at(3))
                    wait(pe, front["xmT"], at(2))
                    transposes(tT, lambda j: xm[:, j], front["xm_t"])
                if is_row(i):
                    pe.wait_ge(front["projT"], at(1))
                    for t in range(T):
                        if t >= 2:
                            pe.wait_ge(f_tanh[t - 2], at(1))
                        elif t == 0:
                            wait(pe, f_tanh[t + 2], at(0))
                        mm(sc[t % 2][:], xnT[:, t * P:(t + 1) * P], projT[:], start=True, stop=True).then_inc(f_score[t], 1)
                if is_row(i - 1):
                    pe.wait_ge(front["xf"], at(0))
                    if i == B:
                        pe.wait_ge(front["scan_x"], at(-1))
                    transposes(misc, lambda j: xf[:, j], front["xf_t"])
                if is_row(i + 2):
                    wait(pe, front["kept"], at(2))
                    transposes(gT, lambda j: gate[:, q, j:j + 1].to_broadcast([P, P]), front["gate_t"])
                if is_row(i):
                    wait(pe, front["h2"], at(0))
                    for t in range(T):
                        pe.wait_ge(f_exp[t], at(1))
                        for j in range(T):
                            dst = o_bank[j // 2][:, j % 2 * ROW:j % 2 * ROW + ROW]
                            last = mm(dst, ex[:, t, j * P:(j + 1) * P], xn[:, q, t, :], start=(t == 0 and j % 2 == 0),
                                      stop=(t == T - 1), skip_group_check=True)
                    last.then_inc(front["att"], 1)

            front_schedule(pe, stages)
            pe.wait_ge(front["scan_x"], B)
            pe.wait_ge(s_scan, 3)

            def acc(dst, w, x, first=False, last=False):
                return mm(dst, w, x, start=first, stop=last, skip_group_check=True)

            def project(gate_n, m, pre, cols):
                units = slice(m * P, (m + 1) * P)
                acc(pre[:, m, :], w_x[:, gate_n, units], scan_x[:, cols], first=(m == 0))
                acc(pre[:, m, :], bias_x[:, gate_n * H + m * P:gate_n * H + (m + 1) * P], ones16[:], last=True)

            def recur(gate_n, pre, k, x):
                for m in range(KC):
                    for c_ in range(KC):
                        for part_ in range(2):
                            last = acc(pre[:, m, k:k + B], w_h[:, part_, gate_n, c_, m * P:(m + 1) * P], x[:, c_, :], last=True)
                return last

            Z, R, C = 0, 1, 2
            for gate_n, pre in ((R, pre_r), (Z, pre_z), (C, pre_c)):
                for m in range(KC):
                    project(gate_n, m, pre[0], slice(0, GC))

            def out_product(o, half, hist):
                acc(pre_o[o], h32[:, hist, o * GC:(o + 1) * GC], w_o[:, hist, :], first=(hist == 0))
                if half == 1:
                    return acc(pre_o[o], ones16[:], bias_o, last=True)

            def scan(at, group, load, first):
                for s in range(BODY):
                    q, k = s // GS, s % GS
                    o, cols = 1 - q, slice(k * B, k * B + B)
                    now = at(s + 1)
                    if k == 0:
                        ahead = at(GS * (q + 1))
                        cols_ahead = slice(ahead * B, ahead * B + GC) if isinstance(ahead, int) else \
                            bass.ds(pe.snap(ahead * B), GC)

                    def side(second):
                        if k == 0:
                            if first and q == 0:
                                return
                            if not second:
                                wait(pe, g["o_sig"], group(q - 2))
                                pe.wait_ge(g["h"], now)
                                out_product(o, 0, 0)
                            else:
                                out_product(o, 1, 1).then_inc(g["o_pre"], 1)
                        else:
                            gate_n, pre = ((R, pre_r), (Z, pre_z), (C, pre_c))[k - 1]
                            project(gate_n, 1 if second else 0, pre[1 - q], cols_ahead)

                    pe.wait_ge(g["u_a"], now)
                    recur(R, pre_r[q], k * B, u_a)
                    pe.wait_ge(g["u_b"], now)
                    recur(R, pre_r[q], k * B, u_b).then_inc(g["r_pre"], 1)
                    pe.wait_ge(g["h_a"], now)
                    recur(Z, pre_z[q], k * B, h_a)
                    pe.wait_ge(g["h_b"], now)
                    recur(Z, pre_z[q], k * B, h_b).then_inc(g["z_pre"], 1)
                    side(False)
                    pe.wait_ge(g["rh_a"], now)
                    recur(C, pre_c[q], k * B, rh_a)
                    pe.wait_ge(g["rh_b"], now)
                    recur(C, pre_c[q], k * B, rh_b).then_inc(g["c_pre"], 1)
                    side(True)
                    q2, k2 = (s + 1) % BODY // GS, (s + 1) % GS * B
                    pe.wait_ge(g["zh_a"], now)
                    recur(R, pre_r[q2], k2, zh_a)
                    pe.wait_ge(g["zh_b"], now)
                    recur(R, pre_r[q2], k2, zh_b)

            scan_schedule(pe, scan)
            wait(pe, g["o_sig"], S // GS - 2)
            pe.wait_ge(g["h"], S + 1)
            out_product(1, 0, 0)
            out_product(1, 1, 1).then_inc(g["o_pre"], 1)


def kernel(**inputs):
    import numpy as np
    import concourse.bacc as bacc
    from concourse.bass_utils import run_bass_kernel_spmd

    a = {k: np.asarray(v) for k, v in inputs.items()}
    f = {k.removeprefix("L0_ffn_"): v for k, v in a.items() if k.startswith("L0_ffn_")}

    def partitions(w):
        return w.reshape(-1, P, w.shape[1]).transpose(1, 0, 2)

    row = np.arange(P)
    consts = np.zeros((P, 2 * P + 7), np.float32)
    consts[:, 0:P] = np.eye(P)
    consts[:, P:2 * P] = row[None, :]
    rows_of_parts = row < 3 * E
    consts[:, 2 * P] = np.where(rows_of_parts, np.where(row % E == 0, -3e38, (D // E) * (row % E) - 1), 3e38)
    for i in range(3):
        consts[:, 2 * P + 1 + i] = rows_of_parts & (row // E == i)
        consts[:, 2 * P + 4 + i] = row == i

    arrays = {
        "x_cols": a["x"].reshape(B * T, P).T,
        "table": np.concatenate([a["L0_tok_emb_table"], a["L0_tok_gate_table"]], axis=1),
        "expert_wT": a["L0_tok_expert_w"].transpose(2, 0, 1),
        "expert_b": a["L0_tok_expert_b"],
        "attn_w": a["L0_attn_attention_weights"],
        "wxT": np.stack([f[n].T for n in ("Wuz", "Wur", "Wu")], axis=1),
        "bx": np.concatenate([f["buz"], f["bur"], f["bu"]])[None],
        "bh": np.concatenate([f["bwz"], f["bwr"], f["bw"]])[None],
        "whT": np.stack([partitions(f[n].T) for n in ("Wwz", "Wwr", "Ww")], axis=1),
        "woT": partitions(f["Wo"].T),
        "bo": f["bo"][None],
        "consts": consts,
    }
    arrays = {k: np.ascontiguousarray(v) for k, v in arrays.items()}
    nc = bacc.Bacc("TRN2", target_bir_lowering=False, num_devices=1)
    args = [nc.dram_tensor(k, v.shape, mybir.dt.from_np(v.dtype), kind="ExternalInput").ap() for k, v in arrays.items()]
    out = nc.dram_tensor("out", (B, S, D), F32, kind="ExternalOutput").ap()
    tower_kernel(nc, *args, out)
    return run_bass_kernel_spmd(nc, [arrays], core_ids=[0]).results[0]["out"]
```

```python
from contextlib import ExitStack

import concourse.bass as bass
from concourse import mybir

F32 = mybir.dt.float32
F16 = mybir.dt.float16
BF16 = mybir.dt.bfloat16
I32 = mybir.dt.int32
U32 = mybir.dt.uint32
ALU = mybir.AluOpType
ACT = mybir.ActivationFunctionType
AX_X = mybir.AxisListType.X
RMAX = bass.bass_isa.ReduceOp.max

P = 128
B, S, D, H, E = 32, 512, 128, 256, 5
T = S // P
ROW = D + 1
KC = H // P
GS = 4
GC = GS * B
BODY = 2 * GS
PACK = 2
BIG = float(2 ** 23)
L_CONST = 1e9
EXPERT_SPAN = D // E
EXPERT_FROM = [float(EXPERT_SPAN * e - 1) for e in range(E)]
EPS = 1e-5
GATE_STEPS = 11
SMALLEST_SCALE = 2.0 ** -12
EXPONENT_BITS = 0x7F800000


def tower_kernel(nc, x_cols, table, expert_wT, expert_b, attn_w, wxT, bx, bh, whT, woT, bo, consts, out):
    h2_dram = nc.dram_tensor("residual_scratch", (B, S, D), F32, kind="Internal").ap()

    with ExitStack() as ctx:
        def sb(name, shape, dt=F32):
            return ctx.enter_context(nc.sbuf_tensor(name, shape, dt))

        def sem(name):
            return ctx.enter_context(nc.semaphore(name))

        bank = [ctx.enter_context(nc.psum_tensor(f"bank{i}", [P, 512], F32)) for i in range(8)]

        const = sb("const", [P, 2 * P + 7])
        ident, unit = const[:, 0:P], const[:, P:2 * P]
        row_from = const[:, 2 * P:2 * P + 1]
        exp_part = [const[:, 2 * P + 1 + i:2 * P + 2 + i] for i in range(3)]
        one_part = [const[:, 2 * P + 4 + i:2 * P + 5 + i] for i in range(3)]
        ones16 = sb("ones16", [P, P], BF16)
        token_id = sb("token_id", [P, B * T], I32)
        w_expert = sb("w_expert", [P, E, D])
        w_expert_in = sb("w_expert_in", [P, E, D])
        w_attn = sb("w_attn", [P, D])
        w_x = sb("w_x", [P, 3, H])
        w_h_in = sb("w_h_in", [P, 3, KC, H])
        w_h = sb("w_h", [P, 2, 3, KC, H], F16)
        w_o_in = sb("w_o_in", [P, KC, D])
        w_o = sb("w_o", [P, KC, D])
        NBIAS = 3 * H + 2 * D
        bias_in = sb("bias_in", [P, NBIAS])
        bias_less = sb("bias_less", [P, NBIAS])
        bias_rest = sb("bias_rest", [P, 3, NBIAS])
        bias_part = sb("bias_part", [P, 3, NBIAS], BF16)
        bias_sum = sb("bias_sum", [P, 3, NBIAS], BF16)
        bias_x, bias_o = bias_sum[:, 2, 0:3 * H], bias_sum[:, 2, 3 * H:3 * H + D]
        bias_e = bias_sum[:, 2, 3 * H + D:NBIAS]
        scales = sb("scales", [P, 8])
        w_max, w_min, w_abs, w_all, w_clamp, h_scale, h_scale2, w_scale = (scales[:, i:i + 1] for i in range(8))
        h_unit = sb("h_unit", [P, KC, B])

        ids_now = sb("ids_now", [P, 2, T], I32)
        emb = sb("emb", [P, 2, T, ROW])
        gate = sb("gate", [P, 2, T])
        frac = sb("frac", [P, 2, T])
        gwork = sb("gwork", [P, 8, T])
        mask = sb("mask", [P, T, P])
        xm = sb("xm", [P, T, P])
        xmT = sb("xmT", [P, T * P])
        kept = sb("kept", [P, E - 1, T * P])
        bias_row = sb("bias_row", [P, T * P], BF16)
        h1 = sb("h1", [P, 2, T, P])
        stat1, stat2 = sb("stat1", [P, T, 6]), sb("stat2", [P, T, 6])
        mv1, mv2 = sb("mv1", [P, T, 2]), sb("mv2", [P, T, 2])
        var1, var2 = sb("var1", [P, T]), sb("var2", [P, T])
        rstd1, rstd2 = sb("rstd1", [P, T]), sb("rstd2", [P, T])
        minus_half = sb("minus_half", [P, T])
        xn = sb("xn", [P, 2, T, ROW])
        xnT = sb("xnT", [P, T * P])
        projT = sb("projT", [P, T * P])
        th = sb("th", [P, T, T * P])
        ex = sb("ex", [P, T, T * P])
        rsum = sb("rsum", [P, T])
        h2 = sb("h2", [P, 2, T, P])
        xf = sb("xf", [P, T, P])
        scan_x = sb("scan_x", [P, (S + GS) * B])

        h32 = sb("h32", [P, KC, BODY * B])
        h_a, h_b = sb("h_a", [P, KC, B], F16), sb("h_b", [P, KC, B], F16)
        r, z, c = sb("r", [P, KC, B]), sb("z", [P, KC, B]), sb("c", [P, KC, B])
        rh, rh_a, rh_b = sb("rh", [P, KC, B]), sb("rh_a", [P, KC, B], F16), sb("rh_b", [P, KC, B], F16)
        zh, zh_a, zh_b = sb("zh", [P, KC, B]), sb("zh_a", [P, KC, B], F16), sb("zh_b", [P, KC, B], F16)
        one_less_z, omz = sb("one_less_z", [P, KC, B]), sb("omz", [P, KC, B])
        u, u_a, u_b = sb("u", [P, KC, B]), sb("u_a", [P, KC, B], F16), sb("u_b", [P, KC, B], F16)
        res = sb("res", [P, 2, D])
        sig = sb("sig", [P, 2, D])
        fin = sb("fin", [P, 2, D])

        s_ids, s_in, s_wh = sem("s_ids"), sem("s_in"), sem("s_wh")
        s_bias_e, s_bias = sem("s_bias_e"), sem("s_bias")
        s_zero, s_dve, s_pool0 = sem("s_zero"), sem("s_dve"), sem("s_pool0")
        s_front, s_max, s_scan = sem("s_front"), sem("s_max"), sem("s_scan")
        front = {n: sem("f_" + n) for n in (
            "ids", "gate0", "gate", "mask", "xm", "xm_t", "gate_t", "xmT", "kept", "bias_row", "y", "h1", "bn1",
            "mv1", "var1", "rstd1", "xn", "xn_t", "xnT", "proj", "projT", "att", "rsum", "h2", "bn2", "mv2", "var2",
            "rstd2", "xf", "xf_t", "scan_x")}
        f_emb = [sem(f"f_emb{i}") for i in range(2)]
        f_store = [sem(f"f_store{i}") for i in range(2)]
        f_score = [sem(f"f_score{t}") for t in range(T)]
        f_tanh = [sem(f"f_tanh{t}") for t in range(T)]
        f_exp = [sem(f"f_exp{t}") for t in range(T)]
        g = {n: sem("g_" + n) for n in ("z_pre", "z", "zh", "zh_a", "zh_b", "one_less_z", "omz", "h", "h_a", "h_b", "o_pre", "o_sig", "o_fin")}
        for n in ("r_pre", "c_pre", "r", "c", "rh", "rh_a", "rh_b", "u", "u_a", "u_b"):
            g[n] = [sem(f"g_{n}{m}") for m in range(KC)]
        o_res = [sem(f"o_res{i}") for i in range(2)]
        o_store = [sem(f"o_store{i}") for i in range(2)]

        tT, gT, sc, y_bank, o_bank, misc = bank[0], bank[1], bank[2:4], bank[4], bank[5:7], bank[7]
        pre_r = [[bank[2 * i + m][:, 0:GC] for m in range(KC)] for i in range(2)]
        pre_c = [[bank[2 * i + m][:, GC:2 * GC] for m in range(KC)] for i in range(2)]
        pre_z = [bank[i][:, 0:KC * GC].rearrange("p (m n) -> p m n", m=KC) for i in (4, 5)]
        pre_o = [bank[i][:, 0:D] for i in (6, 7)]

        def rows(eng, n, per=1, start=0):
            cache = {}

            def at(k):
                if k not in cache:
                    value = n * per + (start + k)
                    cache[k] = value if isinstance(n, int) else eng.snap(value)
                return cache[k]
            return at

        def wait(eng, s, value):
            if not (isinstance(value, int) and value <= 0):
                eng.wait_ge(s, value)

        def wait_apart(eng, s, value, constants, count):
            if not isinstance(value, int):
                value = eng.to_reg(value)
            eng.wait_ge(constants, count)
            wait(eng, s, value)

        def landed(eng, i, at):
            base = at(0)
            if isinstance(base, int):
                return 16 * T * (base // 2 + 1)
            return eng.snap((base - i % 2) * (8 * T) + 16 * T)

        def gate_steps(eng, at, k):
            value = at(0) * GATE_STEPS + k
            return value if isinstance(value, int) else eng.snap(value)

        def stored(eng, i, at):
            base = at(0)
            if isinstance(base, int):
                return 16 * (base // 2)
            return eng.snap((base - i % 2) * 8)

        def front_schedule(eng, stages, scan_constants={}):
            for i in range(-3, 4):
                stages(i, rows(eng, i))
            with eng.Fori(2, B // 2 - 2) as n:
                for p in range(2):
                    stages(4 + p, rows(eng, n, 2, p))
            for i in range(B - 4, B + 1):
                stages(i, rows(eng, i))
                if i in scan_constants:
                    scan_constants[i]()

        def is_row(i):
            return 0 <= i < B

        def scan_schedule(eng, body):
            def pack(n):
                for i in range(PACK):
                    body(rows(eng, n, BODY * PACK, BODY * i), rows(eng, n, 2 * PACK, 2 * i),
                         rows(eng, n, 16 * PACK, 16 * i), isinstance(n, int) and i == 0)

            pack(0)
            with eng.Fori(1, S // BODY // PACK) as n:
                pack(n)

        block = ctx.enter_context(nc.Block())

        @block.sync
        def _(sp):
            sp.dma_start(token_id[:], x_cols).then_inc(s_ids, 16)
            sp.dma_start(const[:], consts).then_inc(s_in, 16)
            sp.dma_start(w_expert_in[:], expert_wT).then_inc(s_in, 16)
            sp.dma_start(w_attn[:], attn_w).then_inc(s_in, 16)
            sp.wait_ge(s_zero, 2)
            xo = slice(3 * H, 3 * H + D)
            xe = slice(3 * H + D, NBIAS)
            for i in range(3):
                sp.dma_start(bias_in[E * i:E * i + E, xe], expert_b).then_inc(s_bias_e, 16)
                sp.dma_start(bias_less[E * i + 1:E * i + E, xe], expert_b[0:E - 1, :]).then_inc(s_bias_e, 16)
            for i in range(3):
                sp.dma_start(bias_in[i:i + 1, 0:3 * H], bx).then_inc(s_bias, 16)
                sp.dma_start(bias_less[i:i + 1, 0:3 * H], bh).then_inc(s_bias, 16)
                sp.dma_start(bias_in[i:i + 1, xo], bo).then_inc(s_bias, 16)
            sp.dma_start(w_x[:], wxT).then_inc(s_wh, 16)
            sp.dma_start(w_h_in[:], whT).then_inc(s_wh, 16)
            sp.dma_start(w_o_in[:], woT).then_inc(s_wh, 16)

            def store_residual(i, at):
                if 0 <= i < B:
                    sp.wait_ge(front["h2"], at(1))
                    dst = h2_dram[bass.ds(at(0), 1), :, :].rearrange("b (j p) d -> p (b j) d", p=P)
                    sp.dma_start(dst, h2[:, i % 2]).then_inc(f_store[i % 2], 16)

            front_schedule(sp, store_residual)
            for i in range(2):
                sp.wait_ge(f_store[i], 16 * (B // 2))

            def rows_of(dram, at, q):
                return dram.rearrange("b s d -> s b d")[bass.ds(at(GS * q), GS), :, :]

            def results(at, group, load, first):
                for q in range(2):
                    if not first:
                        sp.wait_ge(g["o_fin"], group(q - 1))
                        sp.dma_start(rows_before(out, at, q), fin[:, q]).then_inc(o_store[q], 16)
                    sp.dma_start(res[:, q], rows_of(h2_dram, at, q)).then_inc(o_res[q], 16)

            def rows_before(dram, at, q):
                return dram.rearrange("b s d -> s b d")[bass.ds(at(GS * q - BODY), GS), :, :]

            scan_schedule(sp, results)
            for q in range(2):
                sp.wait_ge(g["o_fin"], S // GS - 1 + q)
                sp.dma_start(rows_of(out, lambda k: S - BODY + k, q), fin[:, q]).then_inc(o_store[q], 16)
            for q in range(2):
                sp.wait_ge(o_store[q], 16 * (S // BODY))

        @block.gpsimd
        def _(pool):
            nc.gpsimd.memset(minus_half[:], -0.5).then_inc(s_pool0, 1)
            pool.wait_ge(s_ids, 16)

            def pick_ids(i, at):
                q = i % 2
                nc.gpsimd.tensor_copy(ids_now[:, q], token_id[:, bass.ds(at(0) * T, T)]).then_inc(front["ids"], 1)
                wait_apart(pool, front["ids"], at(1), s_pool0, 1)
                wait(pool, front["xm"], at(-1))

            def gather(i, tiles):
                q = i % 2
                for j in tiles:
                    sent = nc.gpsimd.indirect_dma_start(
                        out=emb[:, q, j, :], out_offset=None, in_=table,
                        in_offset=bass.IndirectOffsetOnAxis(ap=ids_now[:, q, j:j + 1].bitcast(U32), axis=0))
                    sent.then_inc(f_emb[q], 16)

            def gates(i, at):
                q = i % 2
                lands = landed(pool, i, at)
                row_before = at(-1) if isinstance(at(-1), int) else pool.to_reg(at(-1))
                wait_apart(pool, f_emb[q], lands, s_pool0, 1)
                wait(pool, front["gate_t"], row_before)
                ts, tt, w = nc.gpsimd.tensor_scalar, nc.gpsimd.tensor_tensor, gwork
                done = [0]

                def then_wait(ins):
                    done[0] += 1
                    ins.then_inc(front["gate0"], 1)
                    wait_apart(pool, front["gate0"], gate_steps(pool, at, done[0]), s_pool0, 1)

                then_wait(ts(gate[:, q], emb[:, q, :, D], float(D), None, ALU.mult))
                then_wait(ts(w[:, 0], gate[:, q], L_CONST, BIG, ALU.mult, ALU.min))
                then_wait(ts(w[:, 1], w[:, 0], -BIG, None, ALU.max))
                then_wait(ts(w[:, 2], w[:, 1], 0.0, BIG, ALU.max, ALU.add))
                then_wait(ts(w[:, 3], w[:, 1], 0.0, -BIG, ALU.min, ALU.add))
                then_wait(ts(w[:, 3], w[:, 3], BIG, None, ALU.add))
                then_wait(ts(w[:, 2], w[:, 2], -BIG, None, ALU.add))
                then_wait(tt(w[:, 4], w[:, 2], w[:, 3], ALU.add))
                then_wait(tt(w[:, 5], w[:, 4], w[:, 1], ALU.subtract))
                then_wait(ts(w[:, 6], w[:, 5], 0.0, None, ALU.is_gt))
                then_wait(tt(w[:, 7], w[:, 6], w[:, 5], ALU.subtract))
                assert done[0] == GATE_STEPS
                ts(frac[:, q], w[:, 7], 1.0 / L_CONST, None, ALU.mult).then_inc(front["gate"], 1)

            def power(i, at, var, rstd, which, reader):
                pool.wait_ge(front["var" + which], at(1))
                wait(pool, front[reader], at(0))
                nc.gpsimd.tensor_tensor(rstd[:], var[:], minus_half[:], ALU.pow).then_inc(front["rstd" + which], 1)

            def stages(i, at):
                if is_row(i + 2):
                    gates(i + 2, lambda k: at(k + 2))
                if is_row(i + 3):
                    pick_ids(i + 3, lambda k: at(k + 3))
                    gather(i + 3, (0, 1))
                if is_row(i - 1):
                    power(i - 1, lambda k: at(k - 1), var2, rstd2, "2", "xf")
                if is_row(i + 3):
                    gather(i + 3, (2, 3))
                if is_row(i + 1):
                    power(i + 1, lambda k: at(k + 1), var1, rstd1, "1", "xn")

            pool.wait_ge(s_pool0, 1)

            def largest():
                pool.wait_ge(s_max, 3)
                nc.gpsimd.partition_all_reduce(w_all, w_abs, P, RMAX).then_inc(s_max, 1)

            front_schedule(pool, stages, {B - 2: largest})

            def scan(at, group, load, first):
                for s in range(BODY):
                    q = s // GS
                    now = at(s + 1)
                    old = h32[:, :, (s - 1) % BODY * B:(s - 1) % BODY * B + B]
                    pool.wait_ge(g["r"][0], now)
                    pool.wait_ge(g["h"], now)
                    nc.gpsimd.tensor_tensor(rh[:, 0], r[:, 0], old[:, 0], ALU.mult).then_inc(g["rh"][0], 1)
                    pool.wait_ge(g["z"], now)
                    nc.gpsimd.tensor_tensor(zh[:], z[:], old, ALU.mult).then_inc(g["zh"], 1)
                    pool.wait_ge(g["zh"], now)
                    pool.wait_ge(g["zh_a"], now)
                    nc.gpsimd.tensor_tensor(zh_b[:], zh[:], zh_a[:], ALU.subtract).then_inc(g["zh_b"], 1)
                    if s % GS == 1 and not (first and q == 0):
                        output(group(q), load, q)

            def output(count, load, q):
                o = 1 - q
                pool.wait_ge(g["o_sig"], count)
                pool.wait_ge(o_res[o], load(16 if o == 0 else 0))
                wait(pool, o_store[o], load(0 if o == 0 else -16))
                nc.gpsimd.tensor_tensor(fin[:, o], sig[:, o], res[:, o], ALU.add).then_inc(g["o_fin"], 1)

            scan_schedule(pool, scan)
            output(S // GS, lambda k: 16 * (S // BODY) + k, 0)

        @block.scalar
        def _(act):
            def copy(dst, src, s):
                nc.scalar.copy(dst, src).then_inc(s, 1)

            def stages(i, at):
                if is_row(i):
                    act.wait_ge(front["xn_t"], at(1))
                    copy(xnT[:], misc[:], front["xnT"])
                    act.wait_ge(front["proj"], at(1))
                    copy(projT[:], sc[1][:], front["projT"])
                if is_row(i + 1):
                    act.wait_ge(front["y"], at(2))
                    if i >= 1:
                        act.wait_ge(front["h2"], at(0))
                    copy(h1[:, (i + 1) % 2].rearrange("p t d -> p (t d)"), y_bank[:], front["h1"])
                if is_row(i + 2):
                    act.wait_ge(front["xm_t"], at(3))
                    wait(act, front["y"], at(2))
                    copy(xmT[:], tT[:], front["xmT"])
                if is_row(i):
                    for t in range(T + 1):
                        if t < T:
                            act.wait_ge(f_score[t], at(1))
                            nc.scalar.activation(th[:, t], sc[t % 2][:], ACT.Tanh).then_inc(f_tanh[t], 1)
                        if t >= 1:
                            act.wait_ge(f_tanh[t - 1], at(1))
                            nc.scalar.activation(ex[:, t - 1], th[:, t - 1], ACT.Exp).then_inc(f_exp[t - 1], 1)
                if is_row(i - 1):
                    act.wait_ge(front["xf_t"], at(0))
                    dst = scan_x[:, 0:S * B].rearrange("p (s b) -> p s b", b=B)[:, :, bass.ds(at(-1), 1)]
                    copy(dst.rearrange("p s b -> p (s b)"), misc[:], front["scan_x"])

            front_schedule(act, stages)

            def scan(at, group, load, first):
                for s in range(BODY):
                    q, k = s // GS, s % GS * B
                    now = at(s + 1)
                    for m in range(KC):
                        act.wait_ge(g["r_pre"][m], now)
                        nc.scalar.activation(r[:, m], pre_r[q][m][:, k:k + B], ACT.Sigmoid).then_inc(g["r"][m], 1)
                    act.wait_ge(g["z_pre"], now)
                    nc.scalar.activation(one_less_z[:], pre_z[q][:, :, k:k + B], ACT.Sigmoid, scale=-1.0).then_inc(
                        g["one_less_z"], 1)
                    nc.scalar.activation(z[:], pre_z[q][:, :, k:k + B], ACT.Sigmoid).then_inc(g["z"], 1)
                    for m in range(KC):
                        act.wait_ge(g["c_pre"][m], now)
                        nc.scalar.activation(c[:, m], pre_c[q][m][:, k:k + B], ACT.Tanh).then_inc(g["c"][m], 1)
                    if s % GS == 1 and not (first and q == 0):
                        output(group(q), group(q - 2), q)

            def output(count, used, q):
                o = 1 - q
                act.wait_ge(g["o_pre"], count)
                wait(act, g["o_fin"], used)
                nc.scalar.activation(sig[:, o], pre_o[o], ACT.Sigmoid).then_inc(g["o_sig"], 1)

            scan_schedule(act, scan)
            output(S // GS, S // GS - 2, 0)

        @block.vector
        def _(dve):
            v = nc.vector
            done = [0]

            def then_wait(ins):
                done[0] += 1
                ins.then_inc(s_dve, 1)
                dve.wait_ge(s_dve, done[0])

            v.memset(bias_in[:], 0.0).then_inc(s_zero, 1)
            v.memset(bias_less[:], 0.0).then_inc(s_zero, 1)
            v.memset(scan_x[:, S * B:], 0.0).then_inc(s_front, 1)
            v.memset(xn[:, :, :, D:ROW], 1.0).then_inc(s_front, 1)
            v.memset(ones16[:], 1.0).then_inc(s_front, 1)
            dve.wait_ge(s_in, 48)
            v.tensor_copy(w_expert[:, 0], w_expert_in[:, 0]).then_inc(s_front, 1)
            v.tensor_tensor(w_expert[:, 1:E], w_expert_in[:, 1:E], w_expert_in[:, 0:E - 1], ALU.subtract).then_inc(s_front, 1)

            def bias_rows(cols, pick, op):
                then_wait(v.tensor_tensor(bias_rest[:, 0, cols], bias_in[:, cols], bias_less[:, cols], op))
                for k in range(3):
                    then_wait(v.tensor_copy(bias_part[:, k, cols], bias_rest[:, k, cols]))
                    if k < 2:
                        then_wait(v.tensor_tensor(bias_rest[:, k + 1, cols], bias_rest[:, k, cols], bias_part[:, k, cols],
                                                  ALU.subtract))
                then_wait(v.tensor_scalar(bias_sum[:, 0, cols], bias_part[:, 0, cols], pick[0], None, ALU.mult))
                for k in (1, 2):
                    then_wait(v.scalar_tensor_tensor(out=bias_sum[:, k, cols], in0=bias_part[:, k, cols], scalar=pick[k],
                                                     in1=bias_sum[:, k - 1, cols], op0=ALU.mult, op1=ALU.add))

            dve.wait_ge(s_bias_e, 16 * 6)
            bias_rows(slice(3 * H + D, NBIAS), exp_part, ALU.subtract)

            flat = w_h_in[:].rearrange("p a b c -> p (a b c)")

            def gate_biases():
                dve.wait_ge(s_bias, 16 * 9)
                bias_rows(slice(0, 3 * H + D), one_part, ALU.add)

            def weight_magnitudes():
                dve.wait_ge(s_wh, 48)
                v.tensor_reduce(w_max, flat, AX_X, ALU.max).then_inc(s_max, 1)
                v.tensor_reduce(w_min, flat, AX_X, ALU.min).then_inc(s_max, 1)
                dve.wait_ge(s_max, 2)
                v.scalar_tensor_tensor(out=w_abs, in0=w_min, scalar=-1.0, in1=w_max, op0=ALU.mult, op1=ALU.max).then_inc(s_max, 1)
                v.memset(h32[:], 0.0).then_inc(g["h"], 1)
                for t_, s_ in ((h_a, "h_a"), (h_b, "h_b")):
                    v.memset(t_[:], 0.0).then_inc(g[s_], 1)
                for t_, s_ in ((u_a, "u_a"), (u_b, "u_b")):
                    for m in range(KC):
                        v.memset(t_[:, m], 0.0).then_inc(g[s_][m], 1)

            def weight_parts():
                dve.wait_ge(s_max, 4)
                then_wait(v.tensor_scalar(w_clamp, w_all, SMALLEST_SCALE, None, ALU.max))
                then_wait(v.tensor_scalar(h_scale.bitcast(U32), w_clamp.bitcast(U32), EXPONENT_BITS, None, ALU.bitwise_and))
                then_wait(v.tensor_scalar(h_scale2, h_scale, 2.0, None, ALU.mult))
                then_wait(v.reciprocal(w_scale, h_scale2))
                v.tensor_scalar(h_unit[:], unit[:, 0:KC * B].rearrange("p (m n) -> p m n", m=KC), 0.0, h_scale2,
                                ALU.mult, ALU.add).then_inc(s_scan, 1)
                part = w_h[:].rearrange("p s a b c -> p s (a b c)")
                then_wait(v.tensor_scalar(part[:, 0], flat, w_scale, None, ALU.mult))
                v.scalar_tensor_tensor(out=part[:, 1], in0=flat, scalar=w_scale, in1=part[:, 0],
                                       op0=ALU.mult, op1=ALU.subtract).then_inc(s_scan, 1)
                v.tensor_scalar(w_o[:], w_o_in[:], w_scale, None, ALU.mult).then_inc(s_scan, 1)

            def masked(i, at):
                q = i % 2
                dve.wait_ge(front["gate"], at(1))
                dve.wait_ge(f_emb[q], landed(dve, i, at))
                for j in range(T):
                    last = v.tensor_scalar(mask[:, j], unit, gate[:, q, j:j + 1], frac[:, q, j:j + 1], ALU.is_lt, ALU.add)
                last.then_inc(front["mask"], 1)
                dve.wait_ge(front["mask"], at(1))
                wait(dve, front["xm_t"], at(0))
                v.tensor_tensor(xm[:], mask[:], emb[:, q, :, 0:D], ALU.mult).then_inc(front["xm"], 1)

            def residual(i, at):
                q = i % 2
                dve.wait_ge(front["att"], at(1))
                sums = [o_bank[k][:, 0:2 * ROW].rearrange("p (t d) -> p t d", t=2) for k in range(2)]
                v.reciprocal(rsum[:, 0:2], sums[0][:, :, D])
                v.reciprocal(rsum[:, 2:4], sums[1][:, :, D]).then_inc(front["rsum"], 1)
                dve.wait_ge(front["rsum"], at(1))
                wait(dve, f_store[q], stored(dve, i, at))
                for j in range(T):
                    last = v.scalar_tensor_tensor(out=h2[:, q, j], in0=sums[j // 2][:, j % 2, 0:D], scalar=rsum[:, j:j + 1],
                                                  in1=h1[:, q, j], op0=ALU.mult, op1=ALU.add)
                last.then_inc(front["h2"], 1)
                dve.wait_ge(front["h2"], at(1))
                statistics(i, at, h2[:, q], stat2, mv2, var2, "2")

            def statistics(i, at, src, stat, mv, var, which):
                for j in range(T):
                    last = v.bn_stats(stat[:, j], src[:, j])
                last.then_inc(front["bn" + which], 1)
                wait_apart(dve, front["bn" + which], at(1), s_front, 5)
                for j in range(T):
                    last = v.bn_aggr(mv[:, j], stat[:, j])
                last.then_inc(front["mv" + which], 1)
                dve.wait_ge(front["mv" + which], at(1))
                wait(dve, front["rstd" + which], at(0))
                v.tensor_scalar(var[:], mv[:, :, 1], EPS, None, ALU.add).then_inc(front["var" + which], 1)

            def normalise(i, at, dst, src, mv, rstd, which, s):
                dve.wait_ge(front["rstd" + which], at(1))
                for j in range(T):
                    last = v.tensor_scalar(dst[:, j, 0:D], src[:, j], mv[:, j, 0:1], rstd[:, j:j + 1], ALU.subtract, ALU.mult)
                last.then_inc(front[s], 1)

            def experts(i, at):
                dve.wait_ge(front["gate_t"], at(1))
                dve.wait_ge(front["xmT"], at(1))
                wait(dve, front["y"], at(0))
                v.tensor_scalar(bias_row[:], gT[:], row_from, None, ALU.is_gt).then_inc(front["bias_row"], 1)
                for e in range(1, E):
                    last = v.scalar_tensor_tensor(out=kept[:, e - 1], in0=gT[:], scalar=EXPERT_FROM[e], in1=xmT[:],
                                                  op0=ALU.is_gt, op1=ALU.mult)
                last.then_inc(front["kept"], 1)

            def stages(i, at):
                nxt = lambda k: at(k + 1)
                prev = lambda k: at(k - 1)
                if is_row(i - 1):
                    residual(i - 1, prev)
                if is_row(i + 2):
                    masked(i + 2, lambda k: at(k + 2))
                if i == 0:
                    gate_biases()
                if is_row(i - 1):
                    wait(dve, front["xf_t"], prev(0))
                    normalise(i - 1, prev, xf[:], h2[:, (i - 1) % 2], mv2, rstd2, "2", "xf")
                if is_row(i + 1):
                    dve.wait_ge(front["h1"], nxt(1))
                    statistics(i + 1, nxt, h1[:, (i + 1) % 2], stat1, mv1, var1, "1")
                    if i >= 1:
                        dve.wait_ge(front["att"], at(0))
                    normalise(i + 1, nxt, xn[:, (i + 1) % 2], h1[:, (i + 1) % 2], mv1, rstd1, "1", "xn")
                if is_row(i + 2):
                    experts(i + 2, lambda k: at(k + 2))

            front_schedule(dve, stages, {B - 3: weight_magnitudes, B - 1: weight_parts})

            def scan(at, group, load, first):
                for s in range(BODY):
                    q = s // GS
                    now, nxt = at(s + 1), at(s + 2)
                    old = h32[:, :, (s - 1) % BODY * B:(s - 1) % BODY * B + B]
                    new = h32[:, :, s * B:s * B + B]
                    for m in range(KC):
                        dve.wait_ge(g["r"][m], now)
                        v.tensor_tensor(rh_a[:, m], r[:, m], old[:, m], ALU.mult).then_inc(g["rh_a"][m], 1)
                        if m == 1:
                            v.tensor_tensor(rh[:, m], r[:, m], old[:, m], ALU.mult).then_inc(g["rh"][m], 1)
                    for m in range(KC):
                        dve.wait_ge(g["rh"][m], now)
                        if m == 0:
                            dve.wait_ge(g["rh_a"][0], now)
                        v.tensor_tensor(rh_b[:, m], rh[:, m], rh_a[:, m], ALU.subtract).then_inc(g["rh_b"][m], 1)
                    dve.wait_ge(g["one_less_z"], now)
                    v.tensor_tensor(omz[:], one_less_z[:], h_unit[:], ALU.mult).then_inc(g["omz"], 1)
                    dve.wait_ge(g["z"], now)
                    v.tensor_tensor(zh_a[:], z[:], old, ALU.mult).then_inc(g["zh_a"], 1)
                    for m in range(KC):
                        dve.wait_ge(g["c"][m], now)
                        if m == 0:
                            dve.wait_ge(g["omz"], now)
                        v.tensor_tensor(u_a[:, m], c[:, m], omz[:, m], ALU.mult).then_inc(g["u_a"][m], 1)
                        v.tensor_tensor(u[:, m], c[:, m], omz[:, m], ALU.mult).then_inc(g["u"][m], 1)
                    for m in range(KC):
                        dve.wait_ge(g["u"][m], now)
                        v.tensor_tensor(u_b[:, m], u[:, m], u_a[:, m], ALU.subtract).then_inc(g["u_b"][m], 1)
                    dve.wait_ge(g["zh"], now)
                    v.tensor_tensor(h_a[:], u[:], zh[:], ALU.add).then_inc(g["h_a"], 1)
                    v.tensor_tensor(new, u[:], zh[:], ALU.add).then_inc(g["h"], 1)
                    dve.wait_ge(g["h"], nxt)
                    v.tensor_tensor(h_b[:], new, h_a[:], ALU.subtract).then_inc(g["h_b"], 1)

            scan_schedule(dve, scan)

        @block.tensor
        def _(pe):
            mm = nc.tensor.matmul
            pe.wait_ge(s_front, 5)

            def transposes(dst, src, s):
                for j in range(T):
                    last = nc.tensor.transpose(dst[:, j * P:(j + 1) * P], src(j), ident)
                last.then_inc(s, 1)

            def stages(i, at):
                q = i % 2

                def experts(tiles):
                    if tiles[0] == 0:
                        pe.wait_ge(front["bias_row"], at(2))
                        wait(pe, front["h1"], at(1))
                        for j in range(T):
                            cols = slice(j * P, (j + 1) * P)
                            mm(y_bank[:, cols], bias_row[:, cols], bias_e, start=(j == 0), stop=False, skip_group_check=True)
                        pe.wait_ge(front["kept"], at(2))
                    for j in tiles:
                        cols = slice(j * P, (j + 1) * P)
                        for e in range(E):
                            part = xmT if e == 0 else kept[:, e - 1]
                            last = mm(y_bank[:, cols], part[:, cols], w_expert[:, e], start=False, stop=(e == E - 1),
                                      skip_group_check=True)
                    if tiles[-1] == T - 1:
                        last.then_inc(front["y"], 1)

                if is_row(i):
                    pe.wait_ge(front["xn"], at(1))
                    wait(pe, front["scan_x"], at(-1))
                    transposes(misc, lambda j: xn[:, q, j, 0:D], front["xn_t"])
                if is_row(i + 1):
                    experts((0, 1))
                if is_row(i):
                    pe.wait_ge(front["xnT"], at(1))
                    wait(pe, f_tanh[T - 1], at(0))
                    mm(sc[1][:], w_attn[:], xnT[:], start=True, stop=True).then_inc(front["proj"], 1)
                if is_row(i + 1):
                    experts((2, 3))
                if is_row(i + 2):
                    pe.wait_ge(front["xm"], at(3))
                    wait(pe, front["xmT"], at(2))
                    transposes(tT, lambda j: xm[:, j], front["xm_t"])
                if is_row(i):
                    pe.wait_ge(front["projT"], at(1))
                    for t in range(T):
                        if t >= 2:
                            pe.wait_ge(f_tanh[t - 2], at(1))
                        elif t == 0:
                            wait(pe, f_tanh[t + 2], at(0))
                        mm(sc[t % 2][:], xnT[:, t * P:(t + 1) * P], projT[:], start=True, stop=True).then_inc(f_score[t], 1)
                if is_row(i - 1):
                    pe.wait_ge(front["xf"], at(0))
                    if i == B:
                        pe.wait_ge(front["scan_x"], at(-1))
                    transposes(misc, lambda j: xf[:, j], front["xf_t"])
                if is_row(i + 2):
                    wait(pe, front["kept"], at(2))
                    transposes(gT, lambda j: gate[:, q, j:j + 1].to_broadcast([P, P]), front["gate_t"])
                if is_row(i):
                    wait(pe, front["h2"], at(0))
                    for t in range(T):
                        pe.wait_ge(f_exp[t], at(1))
                        for j in range(T):
                            dst = o_bank[j // 2][:, j % 2 * ROW:j % 2 * ROW + ROW]
                            last = mm(dst, ex[:, t, j * P:(j + 1) * P], xn[:, q, t, :], start=(t == 0 and j % 2 == 0),
                                      stop=(t == T - 1), skip_group_check=True)
                    last.then_inc(front["att"], 1)

            front_schedule(pe, stages)
            pe.wait_ge(front["scan_x"], B)
            pe.wait_ge(s_scan, 3)

            def acc(dst, w, x, first=False, last=False):
                return mm(dst, w, x, start=first, stop=last, skip_group_check=True)

            Z, R, C = 0, 1, 2

            def project(gate_n, m, dst, cols, first):
                acc(dst, w_x[:, gate_n, m * P:(m + 1) * P], scan_x[:, cols], first=first)

            def add_bias(gate_n, m, dst):
                acc(dst, bias_x[:, gate_n * H + m * P:gate_n * H + (m + 1) * P], ones16[:], last=True)

            def recur(gate_n, m, c_, pre, x):
                for part_ in range(2):
                    last = acc(pre, w_h[:, part_, gate_n, c_, m * P:(m + 1) * P], x[:, c_, :], last=True)
                return last

            def recur_chunks(gate_n, pre, a, b, s_a, s_b, now, done, between, after, b_order):
                for c_ in range(KC):
                    pe.wait_ge(s_a[c_], now)
                    for m in range(KC):
                        recur(gate_n, m, c_, pre[m], a)
                    if c_ == after:
                        between()
                for c_, m in b_order:
                    if m == 0:
                        pe.wait_ge(s_b[c_], now)
                    last = recur(gate_n, m, c_, pre[m], b)
                    if c_ == KC - 1:
                        last.then_inc(done[m], 1)

            def whole_state(gate_n, pre, x):
                for m in range(KC):
                    for c_ in range(KC):
                        last = recur(gate_n, m, c_, pre[m], x)
                return last

            for m in range(KC):
                for gate_n, dst, opens in ((R, pre_r[0][m], True), (C, pre_c[0][m], False), (Z, pre_z[0][:, m], m == 0)):
                    project(gate_n, m, dst, slice(0, GC), opens)
                    add_bias(gate_n, m, dst)

            def out_product(o, hist):
                acc(pre_o[o], h32[:, hist, o * GC:(o + 1) * GC], w_o[:, hist, :], first=(hist == 0))

            def out_bias(o):
                acc(pre_o[o], ones16[:], bias_o, last=True).then_inc(g["o_pre"], 1)

            def scan(at, group, load, first):
                for s in range(BODY):
                    q, k = s // GS, s % GS
                    o, cols = 1 - q, slice(k * B, k * B + B)
                    now = at(s + 1)
                    r_now = [pre_r[q][m][:, cols] for m in range(KC)]
                    c_now = [pre_c[q][m][:, cols] for m in range(KC)]
                    z_now = [pre_z[q][:, m, cols] for m in range(KC)]

                    if k == 0:
                        ahead = at(GS * (q + 1))
                        cols_ahead = slice(ahead * B, ahead * B + GC) if isinstance(ahead, int) else \
                            bass.ds(pe.snap(ahead * B), GC)
                    outputs = not (first and q == 0)

                    def side(slot):
                        if slot == 0 and outputs:
                            wait(pe, g["o_sig"], group(q - 2))
                            pe.wait_ge(g["h"], now)
                            out_product(o, 0)
                        elif slot == 1 and outputs:
                            out_product(o, 1)
                        elif slot in (2, 3):
                            project(R, slot - 2, pre_r[o][slot - 2], cols_ahead, True)
                        elif slot in (4, 5):
                            project(Z, slot - 4, pre_z[o][:, slot - 4], cols_ahead, slot == 4)
                        elif slot in (6, 7):
                            project(C, slot - 6, pre_c[o][slot - 6], cols_ahead, False)

                    def side_bias(slot):
                        if slot == 1 and outputs:
                            out_bias(o)
                        elif slot in (2, 3):
                            add_bias(R, slot - 2, pre_r[o][slot - 2])
                        elif slot in (4, 5):
                            add_bias(Z, slot - 4, pre_z[o][:, slot - 4])
                        elif slot in (6, 7):
                            add_bias(C, slot - 6, pre_c[o][slot - 6])

                    def rest_of_zh():
                        if not (first and s == 0):
                            pe.wait_ge(g["zh_b"], at(s))
                            whole_state(R, r_now, zh_b)

                    recur_chunks(R, r_now, u_a, u_b, g["u_a"], g["u_b"], now, g["r_pre"], rest_of_zh, 1,
                                 ((0, 0), (1, 0), (0, 1), (1, 1)))
                    if k > 0:
                        side(2 * k)
                    pe.wait_ge(g["h_a"], now)
                    whole_state(Z, z_now, h_a)
                    if k == 0:
                        side(2 * k)
                    pe.wait_ge(g["h_b"], now)
                    last = whole_state(Z, z_now, h_b)
                    last.then_inc(g["z_pre"], 1)
                    pe.wait_ge(g["r"][KC - 1], now)
                    recur_chunks(C, c_now, rh_a, rh_b, g["rh_a"], g["rh_b"], now, g["c_pre"], lambda: side_bias(2 * k), 0,
                                 ((0, 0), (0, 1), (1, 0), (1, 1)))
                    r_next = [pre_r[(s + 1) % BODY // GS][m][:, (s + 1) % GS * B:(s + 1) % GS * B + B] for m in range(KC)]
                    side(2 * k + 1)
                    side_bias(2 * k + 1)
                    pe.wait_ge(g["zh_a"], now)
                    for m in range(KC):
                        pe.wait_ge(g["c"][m], now)
                        for c_ in range(KC):
                            recur(R, m, c_, r_next[m], zh_a)

            scan_schedule(pe, scan)
            pe.wait_ge(g["h"], S + 1)
            for hist in range(KC):
                out_product(1, hist)
            out_bias(1)


def kernel(**inputs):
    import numpy as np
    import concourse.bacc as bacc
    from concourse.bass_utils import run_bass_kernel_spmd

    a = {k: np.asarray(v) for k, v in inputs.items()}
    f = {k.removeprefix("L0_ffn_"): v for k, v in a.items() if k.startswith("L0_ffn_")}

    def partitions(w):
        return w.reshape(-1, P, w.shape[1]).transpose(1, 0, 2)

    row = np.arange(P)
    consts = np.zeros((P, 2 * P + 7), np.float32)
    consts[:, 0:P] = np.eye(P)
    consts[:, P:2 * P] = row[None, :]
    rows_of_parts = row < 3 * E
    consts[:, 2 * P] = np.where(rows_of_parts, np.where(row % E == 0, -3e38, (D // E) * (row % E) - 1), 3e38)
    for i in range(3):
        consts[:, 2 * P + 1 + i] = rows_of_parts & (row // E == i)
        consts[:, 2 * P + 4 + i] = row == i

    arrays = {
        "x_cols": a["x"].reshape(B * T, P).T,
        "table": np.concatenate([a["L0_tok_emb_table"], a["L0_tok_gate_table"]], axis=1),
        "expert_wT": a["L0_tok_expert_w"].transpose(2, 0, 1),
        "expert_b": a["L0_tok_expert_b"],
        "attn_w": a["L0_attn_attention_weights"],
        "wxT": np.stack([f[n].T for n in ("Wuz", "Wur", "Wu")], axis=1),
        "bx": np.concatenate([f["buz"], f["bur"], f["bu"]])[None],
        "bh": np.concatenate([f["bwz"], f["bwr"], f["bw"]])[None],
        "whT": np.stack([partitions(f[n].T) for n in ("Wwz", "Wwr", "Ww")], axis=1),
        "woT": partitions(f["Wo"].T),
        "bo": f["bo"][None],
        "consts": consts,
    }
    arrays = {k: np.ascontiguousarray(v) for k, v in arrays.items()}
    nc = bacc.Bacc("TRN2", target_bir_lowering=False, num_devices=1)
    args = [nc.dram_tensor(k, v.shape, mybir.dt.from_np(v.dtype), kind="ExternalInput").ap() for k, v in arrays.items()]
    out = nc.dram_tensor("out", (B, S, D), F32, kind="ExternalOutput").ap()
    tower_kernel(nc, *args, out)
    return run_bass_kernel_spmd(nc, [arrays], core_ids=[0]).results[0]["out"]
```
